# Optimizing a Trainium2 kernel written in Bass

```python
import numpy as np
import jax
import jax.numpy as jnp

def _softmax(x, axis=-1):
    return jax.nn.softmax(x, axis=axis)

def _gelu(x):
    return jax.nn.gelu(x, approximate=True)

def _silu(x):
    return jax.nn.silu(x)

def _sigmoid(x):
    return jax.nn.sigmoid(x)

def _layernorm(x, axis=-1, eps=1e-05):
    m = jnp.mean(x, axis=axis, keepdims=True)
    v = jnp.var(x, axis=axis, keepdims=True)
    return (x - m) / jnp.sqrt(v + eps)

def _scatter_add(tgt, idx, src, axis=0):
    return tgt.at[idx].add(src)

def _segment_sum(src, seg, n):
    return jax.ops.segment_sum(src, seg, n)
kernel_name = 'mk_xattn_seq_d2_seqx_r8_a2dabd'

def setup_inputs(seed: int=0):
    np.random.seed(seed)
    _w = jnp.asarray

    def _rec_inputs():
        import jax
        import jax.numpy as jnp
        _rk = jax.random.key(seed)
        x = -0.0002928 + 1 * jax.random.normal(jax.random.fold_in(_rk, 1), (128, 64, 128), jnp.float32)
        _lenS = 64 - jax.random.randint(jax.random.fold_in(_rk, 7), (128,), 0, max(1, 64 // 4) + 1, jnp.int32)
        _lenS2 = 64 - jax.random.randint(jax.random.fold_in(_rk, 8), (128,), 0, max(1, 64 // 4) + 1, jnp.int32)
        _ctx_1024P = jax.random.normal(jax.random.fold_in(_rk, 11), (128, 16, 128), jnp.float32)
        _ctx_1024c = jax.random.dirichlet(jax.random.fold_in(_rk, 511), 0.3 * jnp.ones((16,), jnp.float32), (128, 64))
        _ctx_1024t = jnp.einsum('bsk,bkd->bsd', _ctx_1024c, _ctx_1024P)
        _ctx_1024t = _ctx_1024t * jax.lax.rsqrt(jnp.mean(jnp.square(_ctx_1024t)) + 1e-12) * 0.953939
        ctx_1024 = -1.39393e-06 + 0.999914 * (_ctx_1024t + 0.3 * jax.random.normal(jax.random.fold_in(_rk, 611), (128, 64, 128), jnp.float32))
        return (x, ctx_1024)
    x, ctx_1024 = _rec_inputs()

    def _L0_xattn_setup():
        import jax, jax.numpy as jnp
        import numpy as np
        B, S, SE, D, H, FF, E, K = (2, 256, 256, 128, 16, 512, 8, 2)
        HD = D // H

        def _layernorm(x, g, b):
            m = x.mean(-1, keepdims=True)
            v = ((x - m) ** 2).mean(-1, keepdims=True)
            return (x - m) / jnp.sqrt(v + 1e-05) * g + b

        def _attn(q_in, k_in, v_in, wq, bq, wk, bk, wv, bv, wo, bo, causal):
            Bq, Sq, Dm = q_in.shape
            Sk = k_in.shape[1]
            Q = (q_in @ wq + bq).reshape(Bq, Sq, H, HD)
            Kp = (k_in @ wk + bk).reshape(Bq, Sk, H, HD)
            V = (v_in @ wv + bv).reshape(Bq, Sk, H, HD)
            scores = jnp.einsum('bqhd,bkhd->bhqk', Q, Kp) / jnp.sqrt(jnp.float32(HD))
            if causal:
                mask = jnp.tril(jnp.ones((Sq, Sk), bool))
                scores = jnp.where(mask, scores, -jnp.inf)
            a = jax.nn.softmax(scores, axis=-1)
            o = jnp.einsum('bhqk,bkhd->bqhd', a, V).reshape(Bq, Sq, Dm)
            return o @ wo + bo

        def _moe(x, rw, rb, w1, b1, w2, b2):
            T = x.shape[0] * x.shape[1]
            xf = x.reshape(T, D)
            router_weights = jax.nn.softmax(xf @ rw + rb, axis=-1)
            topw, topi = jax.lax.top_k(router_weights, K)
            topw = jax.nn.softmax(topw, axis=-1)
            combine = jnp.zeros((T, E), xf.dtype).at[jnp.arange(T)[:, None], topi].add(topw)
            h = jax.nn.gelu(jnp.einsum('td,edf->etf', xf, w1) + b1[:, None, :], approximate=False)
            eo = jnp.einsum('etf,efd->etd', h, w2) + b2[:, None, :]
            out = jnp.einsum('etd,te->td', eo, combine)
            return out.reshape(x.shape)
        key = jax.random.key(seed)
        ks = jax.random.split(key, 32)
        w = lambda k, shape: jax.random.normal(k, shape, jnp.float32) * 0.02
        inp = {'x': jax.random.normal(ks[0], (B, S, D), jnp.float32), 'encoder_output': jax.random.normal(ks[1], (B, SE, D), jnp.float32), 'sa_wq': w(ks[2], (D, D)), 'sa_bq': jnp.zeros((D,), jnp.float32), 'sa_wk': w(ks[3], (D, D)), 'sa_bk': jnp.zeros((D,), jnp.float32), 'sa_wv': w(ks[4], (D, D)), 'sa_bv': jnp.zeros((D,), jnp.float32), 'sa_wo': w(ks[5], (D, D)), 'sa_bo': jnp.zeros((D,), jnp.float32), 'ca_wq': w(ks[6], (D, D)), 'ca_bq': jnp.zeros((D,), jnp.float32), 'ca_wk': w(ks[7], (D, D)), 'ca_bk': jnp.zeros((D,), jnp.float32), 'ca_wv': w(ks[8], (D, D)), 'ca_bv': jnp.zeros((D,), jnp.float32), 'ca_wo': w(ks[9], (D, D)), 'ca_bo': jnp.zeros((D,), jnp.float32), 'ln1_g': jnp.ones((D,), jnp.float32), 'ln1_b': jnp.zeros((D,), jnp.float32), 'ln2_g': jnp.ones((D,), jnp.float32), 'ln2_b': jnp.zeros((D,), jnp.float32), 'ln3_g': jnp.ones((D,), jnp.float32), 'ln3_b': jnp.zeros((D,), jnp.float32), 'router_w': w(ks[10], (D, E)), 'router_b': jnp.zeros((E,), jnp.float32), 'e_w1': w(ks[11], (E, D, FF)), 'e_b1': jnp.zeros((E, FF), jnp.float32), 'e_w2': w(ks[12], (E, FF, D)), 'e_b2': jnp.zeros((E, D), jnp.float32)}
        return inp
    _L0_xattn_all = _L0_xattn_setup()
    _L0_xattn_in = {k: v for k, v in _L0_xattn_all.items() if k in ('sa_wq', 'sa_bq', 'sa_wk', 'sa_bk', 'sa_wv', 'sa_bv', 'sa_wo', 'sa_bo', 'ca_wq', 'ca_bq', 'ca_wk', 'ca_bk', 'ca_wv', 'ca_bv', 'ca_wo', 'ca_bo', 'ln1_g', 'ln1_b', 'ln2_g', 'ln2_b', 'ln3_g', 'ln3_b', 'router_w', 'router_b', 'e_w1', 'e_b1', 'e_w2', 'e_b2')}
    del _L0_xattn_all

    def _L1_xattn_setup():
        import jax, jax.numpy as jnp
        import numpy as np
        E = 128
        H = 16
        HD = E // H
        EPS = 1e-05

        def _layer_norm(x, g, b):
            mu = jnp.mean(x, axis=-1, keepdims=True)
            var = jnp.var(x, axis=-1, keepdims=True)
            return (x - mu) * jax.lax.rsqrt(var + EPS) * g + b
        key = jax.random.key(seed)
        ks = jax.random.split(key, 16)
        s = 0.02
        inp = {'query': jax.random.normal(ks[0], (4, 128, E), jnp.float32), 'key': jax.random.normal(ks[1], (4, 256, E), jnp.float32), 'value': jax.random.normal(ks[2], (4, 256, E), jnp.float32), 'wq': jax.random.normal(ks[3], (E, E), jnp.float32) * s, 'bq': jnp.zeros((E,), jnp.float32), 'wk': jax.random.normal(ks[4], (E, E), jnp.float32) * s, 'bk': jnp.zeros((E,), jnp.float32), 'wv': jax.random.normal(ks[5], (E, E), jnp.float32) * s, 'bv': jnp.zeros((E,), jnp.float32), 'wo': jax.random.normal(ks[6], (E, E), jnp.float32) * s, 'bo': jnp.zeros((E,), jnp.float32), 'ln1_g': jnp.ones((E,), jnp.float32), 'ln1_b': jnp.zeros((E,), jnp.float32), 'ln2_g': jnp.ones((E,), jnp.float32), 'ln2_b': jnp.zeros((E,), jnp.float32), 'w1': jax.random.normal(ks[7], (E, 4 * E), jnp.float32) * s, 'b1': jnp.zeros((4 * E,), jnp.float32), 'w2': jax.random.normal(ks[8], (4 * E, E), jnp.float32) * s, 'b2': jnp.zeros((E,), jnp.float32)}
        return inp
    _L1_xattn_all = _L1_xattn_setup()
    _L1_xattn_in = {k: v for k, v in _L1_xattn_all.items() if k in ('wq', 'bq', 'wk', 'bk', 'wv', 'bv', 'wo', 'bo', 'ln1_g', 'ln1_b', 'ln2_g', 'ln2_b', 'w1', 'b1', 'w2', 'b2')}
    del _L1_xattn_all
    return {'x': x, 'ctx_1024': ctx_1024, 'L0_xattn_sa_wq': _L0_xattn_in['sa_wq'], 'L0_xattn_sa_bq': _L0_xattn_in['sa_bq'], 'L0_xattn_sa_wk': _L0_xattn_in['sa_wk'], 'L0_xattn_sa_bk': _L0_xattn_in['sa_bk'], 'L0_xattn_sa_wv': _L0_xattn_in['sa_wv'], 'L0_xattn_sa_bv': _L0_xattn_in['sa_bv'], 'L0_xattn_sa_wo': _L0_xattn_in['sa_wo'], 'L0_xattn_sa_bo': _L0_xattn_in['sa_bo'], 'L0_xattn_ca_wq': _L0_xattn_in['ca_wq'], 'L0_xattn_ca_bq': _L0_xattn_in['ca_bq'], 'L0_xattn_ca_wk': _L0_xattn_in['ca_wk'], 'L0_xattn_ca_bk': _L0_xattn_in['ca_bk'], 'L0_xattn_ca_wv': _L0_xattn_in['ca_wv'], 'L0_xattn_ca_bv': _L0_xattn_in['ca_bv'], 'L0_xattn_ca_wo': _L0_xattn_in['ca_wo'], 'L0_xattn_ca_bo': _L0_xattn_in['ca_bo'], 'L0_xattn_ln1_g': _L0_xattn_in['ln1_g'], 'L0_xattn_ln1_b': _L0_xattn_in['ln1_b'], 'L0_xattn_ln2_g': _L0_xattn_in['ln2_g'], 'L0_xattn_ln2_b': _L0_xattn_in['ln2_b'], 'L0_xattn_ln3_g': _L0_xattn_in['ln3_g'], 'L0_xattn_ln3_b': _L0_xattn_in['ln3_b'], 'L0_xattn_router_w': _L0_xattn_in['router_w'], 'L0_xattn_router_b': _L0_xattn_in['router_b'], 'L0_xattn_e_w1': _L0_xattn_in['e_w1'], 'L0_xattn_e_b1': _L0_xattn_in['e_b1'], 'L0_xattn_e_w2': _L0_xattn_in['e_w2'], 'L0_xattn_e_b2': _L0_xattn_in['e_b2'], 'L1_xattn_wq': _L1_xattn_in['wq'], 'L1_xattn_bq': _L1_xattn_in['bq'], 'L1_xattn_wk': _L1_xattn_in['wk'], 'L1_xattn_bk': _L1_xattn_in['bk'], 'L1_xattn_wv': _L1_xattn_in['wv'], 'L1_xattn_bv': _L1_xattn_in['bv'], 'L1_xattn_wo': _L1_xattn_in['wo'], 'L1_xattn_bo': _L1_xattn_in['bo'], 'L1_xattn_ln1_g': _L1_xattn_in['ln1_g'], 'L1_xattn_ln1_b': _L1_xattn_in['ln1_b'], 'L1_xattn_ln2_g': _L1_xattn_in['ln2_g'], 'L1_xattn_ln2_b': _L1_xattn_in['ln2_b'], 'L1_xattn_w1': _L1_xattn_in['w1'], 'L1_xattn_b1': _L1_xattn_in['b1'], 'L1_xattn_w2': _L1_xattn_in['w2'], 'L1_xattn_b2': _L1_xattn_in['b2']}

def reference(x, ctx_1024, L0_xattn_sa_wq, L0_xattn_sa_bq, L0_xattn_sa_wk, L0_xattn_sa_bk, L0_xattn_sa_wv, L0_xattn_sa_bv, L0_xattn_sa_wo, L0_xattn_sa_bo, L0_xattn_ca_wq, L0_xattn_ca_bq, L0_xattn_ca_wk, L0_xattn_ca_bk, L0_xattn_ca_wv, L0_xattn_ca_bv, L0_xattn_ca_wo, L0_xattn_ca_bo, L0_xattn_ln1_g, L0_xattn_ln1_b, L0_xattn_ln2_g, L0_xattn_ln2_b, L0_xattn_ln3_g, L0_xattn_ln3_b, L0_xattn_router_w, L0_xattn_router_b, L0_xattn_e_w1, L0_xattn_e_b1, L0_xattn_e_w2, L0_xattn_e_b2, L1_xattn_wq, L1_xattn_bq, L1_xattn_wk, L1_xattn_bk, L1_xattn_wv, L1_xattn_bv, L1_xattn_wo, L1_xattn_bo, L1_xattn_ln1_g, L1_xattn_ln1_b, L1_xattn_ln2_g, L1_xattn_ln2_b, L1_xattn_w1, L1_xattn_b1, L1_xattn_w2, L1_xattn_b2):
    import jax
    import jax.numpy as jnp

    def _L0_xattn_ref(x, encoder_output, sa_wq, sa_bq, sa_wk, sa_bk, sa_wv, sa_bv, sa_wo, sa_bo, ca_wq, ca_bq, ca_wk, ca_bk, ca_wv, ca_bv, ca_wo, ca_bo, ln1_g, ln1_b, ln2_g, ln2_b, ln3_g, ln3_b, router_w, router_b, e_w1, e_b1, e_w2, e_b2):
        import jax, jax.numpy as jnp
        import numpy as np
        B, S, SE, D, H, FF, E, K = (2, 256, 256, 128, 16, 512, 8, 2)
        HD = D // H

        def _layernorm(x, g, b):
            m = x.mean(-1, keepdims=True)
            v = ((x - m) ** 2).mean(-1, keepdims=True)
            return (x - m) / jnp.sqrt(v + 1e-05) * g + b

        def _attn(q_in, k_in, v_in, wq, bq, wk, bk, wv, bv, wo, bo, causal):
            Bq, Sq, Dm = q_in.shape
            Sk = k_in.shape[1]
            Q = (q_in @ wq + bq).reshape(Bq, Sq, H, HD)
            Kp = (k_in @ wk + bk).reshape(Bq, Sk, H, HD)
            V = (v_in @ wv + bv).reshape(Bq, Sk, H, HD)
            scores = jnp.einsum('bqhd,bkhd->bhqk', Q, Kp) / jnp.sqrt(jnp.float32(HD))
            if causal:
                mask = jnp.tril(jnp.ones((Sq, Sk), bool))
                scores = jnp.where(mask, scores, -jnp.inf)
            a = jax.nn.softmax(scores, axis=-1)
            o = jnp.einsum('bhqk,bkhd->bqhd', a, V).reshape(Bq, Sq, Dm)
            return o @ wo + bo

        def _moe(x, rw, rb, w1, b1, w2, b2):
            T = x.shape[0] * x.shape[1]
            xf = x.reshape(T, D)
            router_weights = jax.nn.softmax(xf @ rw + rb, axis=-1)
            topw, topi = jax.lax.top_k(router_weights, K)
            topw = jax.nn.softmax(topw, axis=-1)
            combine = jnp.zeros((T, E), xf.dtype).at[jnp.arange(T)[:, None], topi].add(topw)
            h = jax.nn.gelu(jnp.einsum('td,edf->etf', xf, w1) + b1[:, None, :], approximate=False)
            eo = jnp.einsum('etf,efd->etd', h, w2) + b2[:, None, :]
            out = jnp.einsum('etd,te->td', eo, combine)
            return out.reshape(x.shape)
        x = _layernorm(x + _attn(x, x, x, sa_wq, sa_bq, sa_wk, sa_bk, sa_wv, sa_bv, sa_wo, sa_bo, True), ln1_g, ln1_b)
        x = _layernorm(x + _attn(x, encoder_output, encoder_output, ca_wq, ca_bq, ca_wk, ca_bk, ca_wv, ca_bv, ca_wo, ca_bo, False), ln2_g, ln2_b)
        x = _layernorm(x + _moe(x, router_w, router_b, e_w1, e_b1, e_w2, e_b2), ln3_g, ln3_b)
        return x

    def _L1_xattn_ref(query, key, value, wq, bq, wk, bk, wv, bv, wo, bo, ln1_g, ln1_b, ln2_g, ln2_b, w1, b1, w2, b2):
        import jax, jax.numpy as jnp
        import numpy as np
        E = 128
        H = 16
        HD = E // H
        EPS = 1e-05

        def _layer_norm(x, g, b):
            mu = jnp.mean(x, axis=-1, keepdims=True)
            var = jnp.var(x, axis=-1, keepdims=True)
            return (x - mu) * jax.lax.rsqrt(var + EPS) * g + b
        B, Sq, _ = query.shape
        Sk = key.shape[1]
        residual = query
        qn = _layer_norm(query, ln1_g, ln1_b)
        kn = _layer_norm(key, ln1_g, ln1_b)
        vn = _layer_norm(value, ln1_g, ln1_b)
        Q = (qn @ wq + bq).reshape(B, Sq, H, HD)
        K = (kn @ wk + bk).reshape(B, Sk, H, HD)
        V = (vn @ wv + bv).reshape(B, Sk, H, HD)
        scores = jnp.einsum('bqhd,bkhd->bhqk', Q, K) / jnp.sqrt(jnp.float32(HD))
        attn = jax.nn.softmax(scores, axis=-1)
        out = jnp.einsum('bhqk,bkhd->bqhd', attn, V).reshape(B, Sq, E)
        out = out @ wo + bo
        x = residual + out
        residual2 = x
        y = _layer_norm(x, ln2_g, ln2_b)
        y = jax.nn.gelu(y @ w1 + b1, approximate=False)
        y = y @ w2 + b2
        return residual2 + y
    x = _L0_xattn_ref(x, ctx_1024, L0_xattn_sa_wq, L0_xattn_sa_bq, L0_xattn_sa_wk, L0_xattn_sa_bk, L0_xattn_sa_wv, L0_xattn_sa_bv, L0_xattn_sa_wo, L0_xattn_sa_bo, L0_xattn_ca_wq, L0_xattn_ca_bq, L0_xattn_ca_wk, L0_xattn_ca_bk, L0_xattn_ca_wv, L0_xattn_ca_bv, L0_xattn_ca_wo, L0_xattn_ca_bo, L0_xattn_ln1_g, L0_xattn_ln1_b, L0_xattn_ln2_g, L0_xattn_ln2_b, L0_xattn_ln3_g, L0_xattn_ln3_b, L0_xattn_router_w, L0_xattn_router_b, L0_xattn_e_w1, L0_xattn_e_b1, L0_xattn_e_w2, L0_xattn_e_b2)
    x = _L1_xattn_ref(x, ctx_1024, ctx_1024, L1_xattn_wq, L1_xattn_bq, L1_xattn_wk, L1_xattn_bk, L1_xattn_wv, L1_xattn_bv, L1_xattn_wo, L1_xattn_bo, L1_xattn_ln1_g, L1_xattn_ln1_b, L1_xattn_ln2_g, L1_xattn_ln2_b, L1_xattn_w1, L1_xattn_b1, L1_xattn_w2, L1_xattn_b2)
    return x

_drawn_inputs = setup_inputs


def setup_inputs(seed=0):
    import zlib

    import numpy as np

    out = dict(_drawn_inputs(seed))
    spreads = {'L0_xattn_sa_bq': (0.0, 0.8),
     'L0_xattn_sa_bk': (0.0, 2.0),
     'L0_xattn_sa_bv': (0.0, 0.272),
     'L0_xattn_sa_bo': (0.0, 0.1),
     'L0_xattn_ca_bq': (0.0, 2.0),
     'L0_xattn_ca_bk': (0.0, 2.0),
     'L0_xattn_ca_bv': (0.0, 0.318),
     'L0_xattn_ca_bo': (0.0, 0.1),
     'L0_xattn_ln1_g': (1.0, 0.2),
     'L0_xattn_ln1_b': (0.0, 0.1),
     'L0_xattn_ln2_g': (1.0, 0.2),
     'L0_xattn_ln2_b': (0.0, 0.1),
     'L0_xattn_ln3_g': (1.0, 0.2),
     'L0_xattn_ln3_b': (0.0, 0.1),
     'L0_xattn_router_b': (0.0, 0.1),
     'L0_xattn_e_b1': (0.0, 0.52),
     'L0_xattn_e_b2': (0.0, 0.1),
     'L1_xattn_bq': (0.0, 2.0),
     'L1_xattn_bk': (0.0, 2.0),
     'L1_xattn_bv': (0.0, 0.403),
     'L1_xattn_bo': (0.0, 0.1),
     'L1_xattn_ln1_g': (1.0, 0.6),
     'L1_xattn_ln1_b': (0.0, 0.8),
     'L1_xattn_ln2_g': (1.0, 0.6),
     'L1_xattn_ln2_b': (0.0, 0.8),
     'L1_xattn_b1': (0.0, 0.354),
     'L1_xattn_b2': (0.0, 0.1)}
    factors = {'L0_xattn_sa_wq': 8.0,
     'L0_xattn_sa_wk': 8.0,
     'L0_xattn_sa_wv': 3.483,
     'L0_xattn_ca_wq': 8.0,
     'L0_xattn_ca_wk': 8.0,
     'L1_xattn_wq': 8.0,
     'L1_xattn_wk': 8.0}
    for name, (base, spread) in spreads.items():
        noise = np.random.default_rng([zlib.crc32(name.encode()), seed]).standard_normal(out[name].shape)
        drawn = base * np.exp(spread * noise) if base else spread * noise
        out[name] = jnp.asarray(drawn.astype(out[name].dtype))
    for name, factor in factors.items():
        out[name] = (out[name] * factor).astype(out[name].dtype)
    return out
```

```python
from contextlib import ExitStack

import concourse.bass as bass
from concourse import mybir

F32 = mybir.dt.float32
BF16 = mybir.dt.bfloat16
ALU = mybir.AluOpType
ACT = mybir.ActivationFunctionType
AX = mybir.AxisListType

P = 128
D = 128
NBATCH, SEQ = 128, 64
T = NBATCH * SEQ
H, HD = 16, 8
J = H // 2
GT = 512
GB = GT // SEQ
GP = GT // P
NG = T // GT
C = J // 2
E, FF = 8, 512
FC = FF // P
SCALE = float(HD) ** -0.5
EPS = 1e-5
MASKED = -1.0e30


def beyond(count, least):
    return not isinstance(count, int) or count > least


def before(count, end):
    return not isinstance(count, int) or count < end


class Names:

    def __init__(self, nc, ctx, prefix):
        self.nc, self.ctx, self.prefix = nc, ctx, prefix
        self.sems = []

    def sb(self, name, shape, dt=F32):
        return self.ctx.enter_context(self.nc.sbuf_tensor(self.prefix + name, shape, dt))

    def ps(self, name, shape, dt=F32):
        return self.ctx.enter_context(self.nc.psum_tensor(self.prefix + name, shape, dt))

    def sem(self, name):
        self.sems.append(self.ctx.enter_context(self.nc.semaphore(self.prefix + name)))
        return self.sems[-1]

    def clear(self):
        for s in self.sems:
            self.nc.gpsimd.sem_clear(s)
        self.nc.all_engine_barrier()


def over_groups(eng, step):
    for u in range(2):
        step(u, u, 0, u == 0, False)
    with eng.Fori(1, NG // 2 - 1) as k:
        for u in range(2):
            step(k * 2 + u, u, k, False, False)
    for u in range(2):
        step(NG - 2 + u, u, NG // 2 - 1, False, u == 1)


class LayerNorm:

    def __init__(self, n, name, y, gain, shift, consts):
        self.y, self.gain, self.shift, self.consts = y, gain, shift, consts
        self.tick = n.sb(name + "_tick", [1, 1])
        self.stats = n.sb(name + "_stats", [P, 2, GP, 6])
        self.mv = n.sb(name + "_mv", [P, 2, GP, 2])
        self.rstd = n.sb(name + "_rstd", [P, 2, GP])
        self.z = n.sb(name + "_z", [P, 2, GP, D])
        self.zg = n.sb(name + "_zg", [P, 2, GP, D])
        self.out = n.sb(name + "_out", [P, 2, GP, D])
        self.stats_ready = n.sem(name + "_stats_ready")
        self.mv_ready = n.sem(name + "_mv_ready")
        self.var_ready = n.sem(name + "_var_ready")
        self.rstd_ready = n.sem(name + "_rstd_ready")
        self.z_ready = n.sem(name + "_z_ready")
        self.zg_ready = n.sem(name + "_zg_ready")
        self.out_ready = n.sem(name + "_out_ready")

    def dve_statistics(self, dve, g, u, k, y_ready, count):
        dve.wait_ge(y_ready, count)
        for t in range(GP):
            ins = dve.bn_stats(self.stats[:, u, t, :], self.y[:, u, t, :])
        ins.then_inc(self.stats_ready, 1)
        dve.wait_ge(self.stats_ready, g + 1)
        if beyond(k, 0):
            dve.wait_ge(self.rstd_ready, g - 1)
        dve.memset(self.tick[:, :], 0.0)
        for t in range(GP):
            ins = dve.bn_aggr(self.mv[:, u, t, :], self.stats[:, u, t, :])
        ins.then_inc(self.mv_ready, 1)

    def pool_rstd(self, pool, g, u, k, first):
        pool.wait_ge(self.mv_ready, g + 1)
        if beyond(k, 0):
            pool.wait_ge(self.z_ready, g - 1)
        pool.tensor_tensor(self.rstd[:, u, :], self.mv[:, u, :, 1], self.consts.eps[:, 0:GP],
                           ALU.add).then_inc(self.var_ready, 1)
        pool.wait_ge(self.var_ready, g + 1)
        pool.tensor_tensor(self.rstd[:, u, :], self.rstd[:, u, :], self.consts.minus_half[:, 0:GP],
                           ALU.pow).then_inc(self.rstd_ready, 1)

    def dve_scale(self, dve, g, u, k, first):
        dve.wait_ge(self.rstd_ready, g + 1)
        dve.wait_ge(self.mv_ready, g + 1)
        if beyond(k, 0):
            dve.wait_ge(self.zg_ready, g - 1)
        for t in range(GP):
            ins = dve.tensor_scalar(self.z[:, u, t, :], self.y[:, u, t, :], self.mv[:, u, t, 0:1],
                                    self.rstd[:, u, t:t + 1], ALU.subtract, ALU.mult)
        ins.then_inc(self.z_ready, 1)

    def pool_gain(self, pool, g, u, k, first, free):
        gain = self.gain[:, None, :].broadcast_to([P, GP, D])
        shift = self.shift[:, None, :].broadcast_to([P, GP, D])
        pool.wait_ge(self.z_ready, g + 1)
        pool.tensor_tensor(self.zg[:, u], self.z[:, u], gain, ALU.mult).then_inc(self.zg_ready, 1)
        pool.wait_ge(self.zg_ready, g + 1)
        free(g, u, k)
        pool.tensor_tensor(self.out[:, u], self.zg[:, u], shift, ALU.add).then_inc(self.out_ready, 1)


def load_constants(nc, n, c, w):
    ld = n.sem("const_loaded")
    made = n.sem("const_made")
    dram = w
    c.ident = n.sb("ident", [P, P])
    c.minus_half = n.sb("minus_half", [P, GP])
    c.eps = n.sb("eps", [P, GP])
    c.side = n.sb("side", [P, 2])
    c.rowi = n.sb("rowi", [P, 1], mybir.dt.int32)
    c.pari = n.sb("pari", [P, 1], mybir.dt.int32)
    c.vx = n.sb("vx", [P, 2, GB, C, D])
    c.kx = n.sb("kx", [P, 2, J, GT])
    c.identb = n.sb("identb", [P, P], BF16)
    c.causal = n.sb("causal", [P, SEQ], BF16)
    c.mat, c.col, c.row = {}, {}, {}
    for name in ("sa_wq", "sa_wk", "sa_wv", "sa_wo", "ca_wq", "ca_wk", "ca_wv", "ca_wo", "l1_wq", "l1_wk",
                 "l1_wv", "l1_wo"):
        c.mat[name] = n.sb(name, [P, D])
    for name in ("sa_bq", "sa_bk", "sa_bv", "ca_bq", "ca_bk", "ca_bv", "l1_bq", "l1_bk", "l1_bv"):
        c.col[name] = n.sb(name, [P, 1])
    for name in ("sa_bo", "ca_bo", "l1_bo", "ln1_g", "ln1_b", "ln2_g", "ln2_b", "ln3_g", "ln3_b", "l1_ln1_g",
                 "l1_ln1_b", "l1_ln2_g", "l1_ln2_b", "l1_b2"):
        c.row[name] = n.sb(name, [P, D])
    c.rw = n.sb("rw", [P, E])
    c.rb = n.sb("rb", [P, E])
    c.eb2 = n.sb("eb2", [E, D])
    c.bqm = n.sb("bqm", [P, 3, 2])
    nloads = len(c.mat) + len(c.col) + len(c.row) + 3

    with nc.Block() as block:
        @block.sync
        def _(sp):
            for name, t in c.mat.items():
                sp.dma_start(t[:, :], dram[name]).then_inc(ld, 16)
            for name, t in c.col.items():
                sp.dma_start(t[:, :], dram[name].rearrange("(p o) -> p o", o=1)).then_inc(ld, 16)
            for name, t in c.row.items():
                sp.dma_start(t[:, :], dram[name].rearrange("(o d) -> o d", o=1).broadcast_to([P, D])).then_inc(ld, 16)
            sp.dma_start(c.rw[:, :], dram["rw"]).then_inc(ld, 16)
            sp.dma_start(c.rb[:, :], dram["rb"].rearrange("(o d) -> o d", o=1).broadcast_to([P, E])).then_inc(ld, 16)
            sp.dma_start(c.eb2[:, :], dram["e_b2"]).then_inc(ld, 16)
            sp.wait_ge(ld, 16 * nloads)

        @block.gpsimd
        def _(pool):
            pool.memset(c.minus_half[:, :], -0.5)
            pool.memset(c.eps[:, :], EPS)
            pool.memset(c.ident[:, :], 0.0).then_inc(made, 1)
            pool.memset(c.causal[:, :], 0.0).then_inc(made, 1)
            pool.iota(c.rowi[:, :], [[0, 1]], base=0, channel_multiplier=1).then_inc(made, 1)
            pool.wait_ge(made, 3)
            pool.affine_select(out=c.ident[:, :], in_=c.ident[:, :], compare_op=ALU.not_equal, fill=1.0, base=0,
                               pattern=[[-1, P]], channel_multiplier=1).then_inc(made, 1)
            for a in range(2):
                pool.wait_ge(made, 4 + a)
                pool.affine_select(out=c.causal[64 * a:64 * a + 64, :], in_=c.causal[64 * a:64 * a + 64, :],
                                   compare_op=ALU.is_ge, fill=MASKED, base=0, pattern=[[-1, SEQ]],
                                   channel_multiplier=1).then_inc(made, 1)

        @block.vector
        def _(dve):
            dve.memset(c.vx[:, :, :, :, :], 0.0)
            dve.memset(c.kx[:, :, :, :], 0.0)
            dve.wait_ge(made, 6)
            dve.tensor_copy(c.identb[:, :], c.ident[:, :])
            dve.tensor_scalar(c.pari[:, :], c.rowi[:, :], 3, 1, ALU.logical_shift_right,
                              ALU.bitwise_and).then_inc(made, 1)
            dve.wait_ge(made, 7)
            dve.tensor_copy(c.side[:, 1:2], c.pari[:, :]).then_inc(made, 1)
            dve.wait_ge(made, 8)
            dve.tensor_scalar(c.side[:, 0:1], c.side[:, 1:2], -1.0, 1.0, ALU.mult, ALU.add).then_inc(made, 1)
            dve.wait_ge(made, 9)
            dve.wait_ge(ld, 16 * nloads)
            for i, name in enumerate(("sa_bq", "ca_bq", "l1_bq")):
                dve.tensor_scalar(c.bqm[:, i, :], c.side[:, :], c.col[name][:, 0:1], None, ALU.mult)


def attention_phase(nc, c, tag, layer, q_src, kv_src, x_src, out_tok, out_tr, causal, gain, shift, store_y):
    wq, wk, wv, wo = (c.mat[f"{layer}_w{m}"] for m in "qkvo")
    bk, bv = c.col[f"{layer}_bk"], c.col[f"{layer}_bv"]
    bo = c.row[f"{layer}_bo"]
    bqm = c.bqm[:, ("sa", "ca", "l1").index(layer), :]
    with ExitStack() as ctx:
        n = Names(nc, ctx, tag)
        qx = n.sb("qx", [P, 2, GT])
        kvx = n.sb("kvx", [P, 2, GB, 2, SEQ])
        xr = n.sb("xr", [P, 2, GP, D])
        xb = n.sb("xb", [P, 2, GP, D])
        kt = n.sb("kt", [P, 2, GT])
        qb = n.sb("qb", [P, 2, GB, 2, SEQ])
        mx = n.sb("mx", [P, 2, J])
        dd = n.sb("dd", [P, 2, J, SEQ])
        pr = n.sb("pr", [P, 2, J, SEQ])
        ph = n.sb("ph", [P, 2, J, SEQ // 2])
        pt = n.sb("pt", [P, 2, C, P])
        su = n.sb("su", [P, 2, 4, J])
        rc = n.sb("rc", [P, 2, 4, J])
        rcx = n.sb("rcx", [P, 2, 4, J, 2 * HD])
        rts = n.sb("rts", [P, 2, 4, 2, SEQ])
        on = n.sb("on", [P, 2, 4, 2, SEQ])
        ot = n.sb("ot", [P, 2, GT])
        y = n.sb("y", [P, 2, GP, D])
        xt = n.sb("xt", [P, 2, GT])
        bob = n.sb("bob", [P, D])
        bvb = n.sb("bvb", [P, P])
        ps_s = [n.ps(f"ps_s{i}", [P, J, SEQ]) for i in range(2)]
        ps_t = [n.ps(f"ps_t{i}", [P, C, P]) for i in range(2)]
        ps_o = [n.ps(f"ps_o{i}", [P, 4, 2, SEQ]) for i in range(2)]
        ps_g = [n.ps(f"ps_g{i}", [P, GT]) for i in range(2)]

        in_q = [n.sem(f"in_q{i}") for i in range(2)]
        in_kv = [n.sem(f"in_kv{i}") for i in range(2)]
        in_x = [n.sem(f"in_x{i}") for i in range(2)]
        kx_in = [n.sem(f"kx_in{i}") for i in range(2)]
        tok_out = [n.sem(f"tok_out{i}") for i in range(2)]
        tr_out = [n.sem(f"tr_out{i}") for i in range(2)]
        bvb_ready, bo_ready, bob_ready = n.sem("bvb_ready"), n.sem("bo_ready"), n.sem("bob_ready")
        k_ready, kt_ready = n.sem("k_ready"), n.sem("kt_ready")
        q_ready, qb_ready = n.sem("q_ready"), n.sem("qb_ready")
        v_ready, vx_ready = n.sem("v_ready"), n.sem("vx_ready")
        s_ready, mx_ready, d_ready = n.sem("s_ready"), n.sem("mx_ready"), n.sem("d_ready")
        p_ready, t_ready, pt_ready = n.sem("p_ready"), n.sem("t_ready"), n.sem("pt_ready")
        pv_ready, ph_ready, su_ready = n.sem("pv_ready"), n.sem("ph_ready"), n.sem("su_ready")
        rcx_ready = n.sem("rcx_ready")
        rc_ready, rt_ready, rts_ready = n.sem("rc_ready"), n.sem("rt_ready"), n.sem("rts_ready")
        on_ready, ot_ready, o_ready = n.sem("on_ready"), n.sem("ot_ready"), n.sem("o_ready")
        xb_ready, y_ready = n.sem("xb_ready"), n.sem("y_ready")
        x_ready, xt_ready = n.sem("x_ready"), n.sem("xt_ready")

        ln = LayerNorm(n, "ln", y, gain, shift, c)
        x_v = x_src.rearrange("(g t p) d -> g p t d", t=GP, p=P)
        tok_v = out_tok.rearrange("(g t p) d -> g p t d", t=GP, p=P)

        with nc.Block() as block:
            @block.sync
            def _(sp):
                def load(g, u, k):
                    if beyond(k, 0):
                        sp.wait_ge(v_ready, 2 * (g - 1))
                        sp.wait_ge(q_ready, g - 1)
                        sp.wait_ge(k_ready, g - 1)
                        sp.wait_ge(xb_ready, g - 1)
                    for e in range(2):
                        sp.dma_start(kvx[:, u, :, e, :], kv_src[:, bass.ts(g, GT)].rearrange(
                            "p (b q) -> p b q", b=GB)).then_inc(in_kv[u], 16)
                    sp.dma_start(qx[:, u, :], q_src[:, bass.ts(g, GT)]).then_inc(in_q[u], 16)
                    sp.dma_start(xr[:, u], x_v[bass.ds(g, 1)].rearrange("o p t d -> p (o t) d")).then_inc(in_x[u], 16)

                def spread(g, u, k):
                    if beyond(k, 0):
                        sp.wait_ge(s_ready, GB * (g - 1))
                    sp.wait_ge(kt_ready, g + 1)
                    for j in range(J):
                        sp.dma_start(c.kx[16 * j:16 * j + 16, u, j, :],
                                     kt[16 * j:16 * j + 16, u, :]).then_inc(kx_in[u], 16)

                def store(g, u, k):
                    if store_y:
                        sp.wait_ge(y_ready, g + 1)
                        src = y
                    else:
                        sp.wait_ge(ln.out_ready, g + 1)
                        src = ln.out
                    sp.dma_start(tok_v[bass.ds(g, 1)].rearrange("o p t d -> p (o t) d"), src[:, u]).then_inc(
                        tok_out[u], 16)
                    sp.wait_ge(xt_ready, g + 1)
                    sp.dma_start(out_tr[:, bass.ts(g, GT)], xt[:, u, :]).then_inc(tr_out[u], 16)

                load(0, 0, 0)
                load(1, 1, 0)
                spread(0, 0, 0)

                def step(g, u, k, first, last):
                    if before(k, NG // 2 - 1):
                        load(g + 2, u, k + 1)
                    if not last:
                        spread(g + 1, 1 - u, k if u == 0 else k + 1)
                    if not first:
                        store(g - 1, 1 - u, k)
                over_groups(sp, step)
                store(NG - 1, 1, NG // 2)
                for u in range(2):
                    sp.wait_ge(tok_out[u], 16 * (NG // 2))
                    sp.wait_ge(tr_out[u], 16 * (NG // 2))

            @block.tensor
            def _(pe):
                def scores(g, b, u, k):
                    nb = g * GB + b
                    if b == 0:
                        pe.wait_ge(kx_in[u], 16 * J * (k + 1))
                        pe.wait_ge(qb_ready, g + 1)
                    if beyond(nb, 1):
                        pe.wait_ge(d_ready, nb - 1)
                    mm = pe.matmul(ps_s[b % 2][:, :, :], qb[:, u, b, :, :], c.kx[:, u, :, 64 * b:64 * b + 64],
                                   start=True, stop=not causal)
                    if causal:
                        mm = pe.matmul(ps_s[b % 2][:, :, :], c.identb[:, :],
                                       c.causal[:, None, :].broadcast_to([P, J, SEQ]), start=False, stop=True)
                    mm.then_inc(s_ready, 1)

                def turn(g, b):
                    nb = g * GB + b
                    pe.wait_ge(p_ready, nb + 1)
                    if beyond(nb, 1):
                        pe.wait_ge(pt_ready, nb - 1)
                    for q in range(C):
                        tr = pe.transpose(ps_t[b % 2][:, q, :], pr[:, b % 2, 2 * q:2 * q + 2, :], c.ident[:, :])
                    tr.then_inc(t_ready, 1)

                def values(g, b, u):
                    nb = g * GB + b
                    quad = g * 2 + b // 4
                    pe.wait_ge(pt_ready, nb + 1)
                    if b == 0:
                        pe.wait_ge(vx_ready, 2 * g + 2)
                    if b % 4 == 0 and beyond(quad, 1):
                        pe.wait_ge(on_ready, quad - 1)
                    for q in range(C):
                        mm = pe.matmul(ps_o[b // 4][:, b % 4, :, :], c.vx[:, u, b, q, :], pt[:, b % 2, q, :],
                                       start=(q == 0), stop=(q == C - 1))
                    mm.then_inc(pv_ready, 1)

                def project_k(g, u, k, first):
                    pe.wait_ge(in_kv[u], 32 * (k + 1))
                    if not first:
                        pe.wait_ge(rts_ready, 2 * (g - 1) - 1)
                    pe.matmul(ps_g[0][:, :], wk[:, :], kvx[:, u, :, 0, :], start=True, stop=True).then_inc(k_ready, 1)

                def project_q(g, u, k, first):
                    pe.wait_ge(in_q[u], 16 * (k + 1))
                    pe.wait_ge(kt_ready, g + 1)
                    pe.matmul(ps_g[0][:, :], wq[:, :], qx[:, u, :], start=True, stop=True).then_inc(q_ready, 1)

                def project_v(g, u, half, bank):
                    for b in range(4):
                        mm = pe.matmul(ps_g[bank][:, D * b:D * b + D], kvx[:, u, 4 * half + b, :, :], wv[:, :],
                                       start=True, stop=True)
                    mm.then_inc(v_ready, 1)

                def reciprocals(quad, qu, bank):
                    pe.wait_ge(rcx_ready, quad + 1)
                    for b in range(4):
                        mm = pe.matmul(ps_g[bank][:, P * b:P * b + P],
                                       rcx[:, qu, b, :, :], c.ident[:, :],
                                       start=True, stop=True)
                    mm.then_inc(rt_ready, 1)

                def project_out(g, u):
                    pe.wait_ge(ot_ready, 2 * g + 2)
                    for t in range(GP):
                        mm = pe.matmul(ps_g[1][:, D * t:D * t + D], ot[:, u, P * t:P * t + P], wo[:, :],
                                       start=True, stop=True)
                    mm.then_inc(o_ready, 1)

                def turn_x(g, u):
                    pe.wait_ge(ln.out_ready, g + 1)
                    for t in range(GP):
                        tr = pe.transpose(ps_g[1][:, P * t:P * t + P], ln.out[:, u, t, :], c.ident[:, :])
                    tr.then_inc(x_ready, 1)

                pe.wait_ge(bvb_ready, 1)
                pe.matmul(ps_g[1][:, 0:D], bvb[:, :], wo[:, :], start=True, stop=True).then_inc(bo_ready, 1)
                project_k(0, 0, 0, True)
                project_q(0, 0, 0, True)
                pe.wait_ge(bob_ready, 1)
                project_v(0, 0, 0, 1)
                pe.wait_ge(qb_ready, 1)
                project_v(0, 0, 1, 0)
                scores(0, 0, 0, 0)

                def step(g, u, k, first, last):
                    k1 = k if u == 0 else k + 1
                    for b in range(GB):
                        if b < GB - 1:
                            scores(g, b + 1, u, k)
                        elif not last:
                            scores(g + 1, 0, 1 - u, k1)
                        turn(g, b)
                        if b > 0:
                            values(g, b - 1, u)
                        elif not first:
                            values(g - 1, GB - 1, 1 - u)
                        if b == 0 and not last:
                            if first:
                                pe.wait_ge(vx_ready, 2)
                            project_k(g + 1, 1 - u, k1, first)
                        if b == 1:
                            if not last:
                                project_q(g + 1, 1 - u, k1, first)
                            if not first:
                                if beyond(g, 1):
                                    pe.wait_ge(xt_ready, g - 1)
                                reciprocals(2 * g - 1, 1, 1)
                        if b == 2 and not last:
                            if first:
                                pe.wait_ge(vx_ready, 1)
                            else:
                                pe.wait_ge(rts_ready, 2 * g)
                            project_v(g + 1, 1 - u, 0, 1)
                        if b == 3 and not last:
                            pe.wait_ge(qb_ready, g + 2)
                            project_v(g + 1, 1 - u, 1, 0)
                        if b == 4 and not first:
                            if last:
                                pe.wait_ge(rts_ready, 2 * g)
                            else:
                                pe.wait_ge(vx_ready, 2 * g + 3)
                            project_out(g - 1, 1 - u)
                        if b == 5:
                            if last:
                                pe.wait_ge(rts_ready, 2 * g - 1)
                            else:
                                pe.wait_ge(vx_ready, 2 * g + 4)
                            reciprocals(2 * g, 0, 0)
                        if b == 7 and not first:
                            pe.wait_ge(y_ready, g)
                            turn_x(g - 1, 1 - u)
                over_groups(pe, step)
                values(NG - 1, GB - 1, 1)
                pe.wait_ge(xt_ready, NG - 1)
                reciprocals(2 * NG - 1, 1, 1)
                pe.wait_ge(rts_ready, 2 * NG)
                project_out(NG - 1, 1)
                pe.wait_ge(y_ready, NG)
                turn_x(NG - 1, 1)

            @block.scalar
            def _(act):
                def copy_q(g, u, k):
                    act.wait_ge(q_ready, g + 1)
                    if beyond(k, 0):
                        act.wait_ge(s_ready, GB * (g - 1))
                    for a in range(2):
                        ins = act.activation(qb[:, u, :, a, :], ps_g[0][:, :].rearrange("p (b q) -> p b q", b=GB),
                                             ACT.Identity, bias=bqm[:, a:a + 1], scale=c.side[:, a:a + 1])
                    ins.then_inc(qb_ready, 1)

                def copy_v(g, u, k, half, bank):
                    act.wait_ge(v_ready, 2 * g + half + 1)
                    if half == 0 and beyond(k, 0):
                        act.wait_ge(pv_ready, GB * (g - 1))
                    for r in range(2):
                        src = ps_g[bank][64 * r:64 * r + 64, :].rearrange(
                            "p (b c r m) -> p b c r m", b=4, c=C, r=2)[:, :, :, r, :]
                        dst = c.vx[64 * r:64 * r + 64, u, 4 * half:4 * half + 4, :, :].rearrange(
                            "p b c (e r m) -> p b (c e) r m", r=2, m=16)[:, :, 0:C * C:C + 1, r, :]
                        ins = act.activation(dst, src, ACT.Copy)
                    ins.then_inc(vx_ready, 1)

                def exponent(g, b):
                    nb = g * GB + b
                    act.wait_ge(d_ready, nb + 1)
                    if beyond(nb, 1):
                        act.wait_ge(t_ready, nb - 1)
                        act.wait_ge(ph_ready, nb - 1)
                    act.activation(pr[:, b % 2], dd[:, b % 2], ACT.Exp, scale=SCALE).then_inc(p_ready, 1)

                def copy_t(g, b):
                    nb = g * GB + b
                    act.wait_ge(t_ready, nb + 1)
                    if beyond(nb, 1):
                        act.wait_ge(pv_ready, nb - 1)
                    act.activation(pt[:, b % 2], ps_t[b % 2][:, :, :], ACT.Copy).then_inc(pt_ready, 1)

                def widen_r(quad, qu):
                    act.wait_ge(rc_ready, quad + 1)
                    if beyond(quad, 1):
                        act.wait_ge(rt_ready, quad - 1)
                    act.activation(rcx[:, qu], rc[:, qu, :, :, None].broadcast_to([P, 4, J, 2 * HD]),
                                   ACT.Copy).then_inc(rcx_ready, 1)

                def copy_r(quad, qu, bank):
                    act.wait_ge(rt_ready, quad + 1)
                    if beyond(quad, 1):
                        act.wait_ge(on_ready, quad - 1)
                    src = ps_g[bank][:, :].rearrange("p (b a q) -> p b a q", b=4, a=2)
                    for a in range(2):
                        ins = act.activation(rts[:, qu, :, a, :], src[:, :, a, :], ACT.Copy,
                                             scale=c.side[:, a:a + 1])
                    ins.then_inc(rts_ready, 1)

                def copy_x(g, u, k):
                    act.wait_ge(x_ready, g + 1)
                    if beyond(k, 0):
                        act.wait_ge(tr_out[u], 16 * k)
                    act.activation(xt[:, u, :], ps_g[1][:, :], ACT.Copy).then_inc(xt_ready, 1)

                copy_q(0, 0, 0)
                copy_v(0, 0, 0, 0, 1)
                copy_v(0, 0, 0, 1, 0)
                exponent(0, 0)

                def step(g, u, k, first, last):
                    k1 = k if u == 0 else k + 1
                    for b in range(GB):
                        copy_t(g, b)
                        if b < GB - 1:
                            exponent(g, b + 1)
                        elif not last:
                            exponent(g + 1, 0)
                        if b == 0 and not first:
                            widen_r(2 * g - 1, 1)
                        if b == 4:
                            widen_r(2 * g, 0)
                        if b == 1:
                            if not last:
                                copy_q(g + 1, 1 - u, k1)
                            if not first:
                                copy_r(2 * g - 1, 1, 1)
                        if b == 2 and not last:
                            copy_v(g + 1, 1 - u, k1, 0, 1)
                        if b == 3 and not last:
                            copy_v(g + 1, 1 - u, k1, 1, 0)
                        if b == 5:
                            copy_r(2 * g, 0, 0)
                        if b == 7 and not first:
                            copy_x(g - 1, 1 - u, k if u == 1 else k - 1)
                over_groups(act, step)
                widen_r(2 * NG - 1, 1)
                copy_r(2 * NG - 1, 1, 1)
                copy_x(NG - 1, 1, NG // 2 - 1)

            @block.vector
            def _(dve):
                def copy_k(g, u, k):
                    dve.wait_ge(k_ready, g + 1)
                    if beyond(k, 0):
                        dve.wait_ge(kx_in[u], 16 * J * k)
                    dve.tensor_scalar(kt[:, u, :], ps_g[0][:, :], bk[:, 0:1], None, ALU.add).then_inc(kt_ready, 1)

                def shift_scores(g, b):
                    nb = g * GB + b
                    dve.wait_ge(s_ready, nb + 1)
                    dve.tensor_reduce(mx[:, b % 2, :], ps_s[b % 2][:, :, :], AX.X, ALU.max).then_inc(mx_ready, 1)
                    dve.wait_ge(mx_ready, nb + 1)
                    if beyond(nb, 1):
                        dve.wait_ge(p_ready, nb - 1)
                    dve.tensor_tensor(dd[:, b % 2], ps_s[b % 2][:, :, :],
                                      mx[:, b % 2, :, None].broadcast_to([P, J, SEQ]),
                                      ALU.subtract).then_inc(d_ready, 1)

                def sum_up(g, b):
                    nb = g * GB + b
                    dve.wait_ge(ph_ready, nb + 1)
                    dve.tensor_reduce(su[:, b // 4, b % 4, :], ph[:, b % 2], AX.X, ALU.add).then_inc(su_ready, 1)

                def recip(quad, qu):
                    dve.wait_ge(su_ready, 4 * quad + 4)
                    if beyond(quad, 1):
                        dve.wait_ge(rcx_ready, quad - 1)
                    dve.reciprocal(rc[:, qu], su[:, qu]).then_inc(rc_ready, 1)

                def normalise(quad, qu):
                    dve.wait_ge(rts_ready, quad + 1)
                    dve.wait_ge(pv_ready, 4 * quad + 4)
                    if beyond(quad, 1):
                        dve.wait_ge(ot_ready, quad - 1)
                    dve.tensor_tensor(on[:, qu], ps_o[qu][:, :, :, :], rts[:, qu], ALU.mult).then_inc(on_ready, 1)

                def residual(g, u, k):
                    dve.wait_ge(o_ready, g + 1)
                    dve.wait_ge(xb_ready, g + 1)
                    if store_y and beyond(k, 0):
                        dve.wait_ge(tok_out[u], 16 * k)
                    dve.tensor_tensor(y[:, u], ps_g[1][:, :].rearrange("p (t d) -> p t d", t=GP), xb[:, u],
                                      ALU.add).then_inc(y_ready, 1)

                dve.tensor_copy(bvb[:, :], bv[:, 0:1].broadcast_to([P, P])).then_inc(bvb_ready, 1)
                dve.wait_ge(bo_ready, 1)
                dve.tensor_tensor(bob[:, :], ps_g[1][:, 0:D], bo[:, :], ALU.add).then_inc(bob_ready, 1)
                copy_k(0, 0, 0)
                shift_scores(0, 0)

                def step(g, u, k, first, last):
                    k1 = k if u == 0 else k + 1
                    kp = k if u == 1 else k - 1
                    for b in range(GB):
                        if b < GB - 1:
                            shift_scores(g, b + 1)
                        elif not last:
                            shift_scores(g + 1, 0)
                        sum_up(g, b)
                        if b == 0:
                            if not last:
                                copy_k(g + 1, 1 - u, k1)
                        if b == 2 and not first:
                            normalise(2 * g - 1, 1)
                        if b == 3:
                            recip(2 * g, 0)
                        if b == 4 and not first:
                            residual(g - 1, 1 - u, kp)
                            ln.dve_statistics(dve, g - 1, 1 - u, kp, y_ready, g)
                        if b == 5 and not first:
                            ln.dve_scale(dve, g - 1, 1 - u, kp, first)
                        if b == 6:
                            normalise(2 * g, 0)
                        if b == 7:
                            recip(2 * g + 1, 1)
                over_groups(dve, step)
                normalise(2 * NG - 1, 1)
                residual(NG - 1, 1, NG // 2 - 1)
                ln.dve_statistics(dve, NG - 1, 1, NG // 2 - 1, y_ready, NG)
                ln.dve_scale(dve, NG - 1, 1, NG // 2 - 1, False)

            @block.gpsimd
            def _(pool):
                def halve(g, b):
                    nb = g * GB + b
                    pool.wait_ge(p_ready, nb + 1)
                    if beyond(nb, 1):
                        pool.wait_ge(su_ready, nb - 1)
                    pool.tensor_tensor(ph[:, b % 2], pr[:, b % 2, :, 0:SEQ // 2], pr[:, b % 2, :, SEQ // 2:SEQ],
                                       ALU.add).then_inc(ph_ready, 1)

                def add_bias(g, u, k):
                    pool.wait_ge(in_x[u], 16 * (k + 1))
                    if beyond(k, 0):
                        pool.wait_ge(y_ready, g - 1)
                    pool.tensor_tensor(xb[:, u], xr[:, u], bob[:, None, :].broadcast_to([P, GP, D]),
                                       ALU.add).then_inc(xb_ready, 1)

                def gather(quad, qu, g, u, k):
                    pool.wait_ge(on_ready, quad + 1)
                    if beyond(k, 0):
                        pool.wait_ge(o_ready, g - 1)
                    pool.tensor_tensor(ot[:, u, 256 * qu:256 * qu + 256].rearrange("p (b q) -> p b q", b=4),
                                       on[:, qu, :, 0, :], on[:, qu, :, 1, :], ALU.add).then_inc(ot_ready, 1)

                def out_free(g, u, k):
                    if beyond(k, 0):
                        pool.wait_ge(x_ready, g - 1)
                        if not store_y:
                            pool.wait_ge(tok_out[u], 16 * k)

                pool.wait_ge(bob_ready, 1)
                add_bias(0, 0, 0)

                def step(g, u, k, first, last):
                    k1 = k if u == 0 else k + 1
                    kp = k if u == 1 else k - 1
                    for b in range(GB):
                        halve(g, b)
                        if b == 2 and not first:
                            gather(2 * g - 1, 1, g - 1, 1 - u, kp)
                        if b == 4 and not first:
                            ln.pool_rstd(pool, g - 1, 1 - u, kp, first)
                        if b == 5 and not last:
                            add_bias(g + 1, 1 - u, k1)
                        if b == 6:
                            if not first:
                                ln.pool_gain(pool, g - 1, 1 - u, kp, first, out_free)
                            gather(2 * g, 0, g, u, k)
                over_groups(pool, step)
                gather(2 * NG - 1, 1, NG - 1, 1, NG // 2 - 1)
                ln.pool_rstd(pool, NG - 1, 1, NG // 2 - 1, False)
                ln.pool_gain(pool, NG - 1, 1, NG // 2 - 1, False, out_free)
        n.clear()


def norm_phase(nc, c, tag, src_tok, out_tr, gain, shift):
    with ExitStack() as ctx:
        n = Names(nc, ctx, tag)
        xr = n.sb("xr", [P, 2, GP, D])
        y = n.sb("y", [P, 2, GP, D])
        xt = n.sb("xt", [P, 2, GT])
        ps_x = [n.ps(f"ps_x{i}", [P, GT]) for i in range(2)]
        in_x = [n.sem(f"in_x{i}") for i in range(2)]
        tr_out = [n.sem(f"tr_out{i}") for i in range(2)]
        y_ready, x_ready, xt_ready = n.sem("y_ready"), n.sem("x_ready"), n.sem("xt_ready")
        ln = LayerNorm(n, "ln", y, gain, shift, c)
        x_v = src_tok.rearrange("(g t p) d -> g p t d", t=GP, p=P)

        with nc.Block() as block:
            @block.sync
            def _(sp):
                def load(g, u, k):
                    if beyond(k, 0):
                        sp.wait_ge(y_ready, g - 1)
                    sp.dma_start(xr[:, u], x_v[bass.ds(g, 1)].rearrange("o p t d -> p (o t) d")).then_inc(in_x[u], 16)

                def step(g, u, k, first, last):
                    if before(k, NG // 2 - 1):
                        load(g + 2, u, k + 1)
                    sp.wait_ge(xt_ready, g + 1)
                    sp.dma_start(out_tr[:, bass.ts(g, GT)], xt[:, u, :]).then_inc(tr_out[u], 16)
                load(0, 0, 0)
                load(1, 1, 0)
                over_groups(sp, step)
                for u in range(2):
                    sp.wait_ge(tr_out[u], 16 * (NG // 2))

            @block.tensor
            def _(pe):
                def step(g, u, k, first, last):
                    pe.wait_ge(ln.out_ready, g + 1)
                    if beyond(k, 0):
                        pe.wait_ge(xt_ready, g - 1)
                    for t in range(GP):
                        tr = pe.transpose(ps_x[u][:, P * t:P * t + P], ln.out[:, u, t, :], c.ident[:, :])
                    tr.then_inc(x_ready, 1)
                over_groups(pe, step)

            @block.scalar
            def _(act):
                def copy_in(g, u, k):
                    act.wait_ge(in_x[u], 16 * (k + 1))
                    if beyond(k, 0):
                        act.wait_ge(ln.z_ready, g - 1)
                    act.activation(y[:, u], xr[:, u], ACT.Copy).then_inc(y_ready, 1)

                def step(g, u, k, first, last):
                    if not last:
                        copy_in(g + 1, 1 - u, k if u == 0 else k + 1)
                    act.wait_ge(x_ready, g + 1)
                    if beyond(k, 0):
                        act.wait_ge(tr_out[u], 16 * k)
                    act.activation(xt[:, u, :], ps_x[u][:, :], ACT.Copy).then_inc(xt_ready, 1)
                copy_in(0, 0, 0)
                over_groups(act, step)

            @block.vector
            def _(dve):
                def step(g, u, k, first, last):
                    ln.dve_statistics(dve, g, u, k, y_ready, g + 1)
                    if not first:
                        ln.dve_scale(dve, g - 1, 1 - u, k if u == 1 else k - 1, first)
                over_groups(dve, step)
                ln.dve_scale(dve, NG - 1, 1, NG // 2 - 1, False)

            @block.gpsimd
            def _(pool):
                def free(g, u, k):
                    if beyond(k, 0):
                        pool.wait_ge(x_ready, g - 1)

                def step(g, u, k, first, last):
                    ln.pool_rstd(pool, g, u, k, first)
                    if not first:
                        ln.pool_gain(pool, g - 1, 1 - u, k if u == 1 else k - 1, first, free)
                over_groups(pool, step)
                ln.pool_gain(pool, NG - 1, 1, NG // 2 - 1, False, free)
        n.clear()


def mlp_phase(nc, c, tag, xt_src, x_src, w1_dram, b1_dram, w2_dram, b2, out_tok):
    with ExitStack() as ctx:
        n = Names(nc, ctx, tag)
        w1 = n.sb("w1", [P, FF])
        w2 = n.sb("w2", [P, FC, D])
        b1 = n.sb("b1", [P, FC])
        xt = n.sb("xt", [P, 2, GT])
        xr = n.sb("xr", [P, 2, GP, D])
        xb = n.sb("xb", [P, 2, GP, D])
        hid = n.sb("hid", [P, 2, GT])
        y = n.sb("y", [P, 2, GP, D])
        ps_h = [n.ps(f"ps_h{i}", [P, GT]) for i in range(2)]
        ps_y = [n.ps(f"ps_y{i}", [P, GP, D]) for i in range(2)]
        ld = n.sem("weights_loaded")
        in_t = [n.sem(f"in_t{i}") for i in range(2)]
        in_x = [n.sem(f"in_x{i}") for i in range(2)]
        y_out = [n.sem(f"y_out{i}") for i in range(2)]
        h_ready, hid_ready, o_ready = n.sem("h_ready"), n.sem("hid_ready"), n.sem("o_ready")
        used, xb_ready, y_ready = n.sem("hid_used"), n.sem("xb_ready"), n.sem("y_ready")
        x_v = x_src.rearrange("(g t p) d -> g p t d", t=GP, p=P)
        out_v = out_tok.rearrange("(g t p) d -> g p t d", t=GP, p=P)

        with nc.Block() as block:
            @block.sync
            def _(sp):
                sp.dma_start(w1[:, :], w1_dram).then_inc(ld, 16)
                sp.dma_start(w2[:, :, :], w2_dram.rearrange("(c p) d -> p c d", p=P)).then_inc(ld, 16)
                sp.dma_start(b1[:, :], b1_dram).then_inc(ld, 16)

                def load(g, u, k):
                    if beyond(k, 0):
                        sp.wait_ge(h_ready, FC * (g - 1))
                        sp.wait_ge(xb_ready, g - 1)
                    sp.dma_start(xt[:, u, :], xt_src[:, bass.ts(g, GT)]).then_inc(in_t[u], 16)
                    sp.dma_start(xr[:, u], x_v[bass.ds(g, 1)].rearrange("o p t d -> p (o t) d")).then_inc(in_x[u], 16)

                def step(g, u, k, first, last):
                    if before(k, NG // 2 - 1) and not first:
                        load(g + 1, 1 - u, k if u == 0 else k + 1)
                    elif not first and not last:
                        load(g + 1, 1 - u, k if u == 0 else k + 1)
                    sp.wait_ge(y_ready, g + 1)
                    sp.dma_start(out_v[bass.ds(g, 1)].rearrange("o p t d -> p (o t) d"), y[:, u]).then_inc(
                        y_out[u], 16)
                load(0, 0, 0)
                load(1, 1, 0)
                over_groups(sp, step)
                for u in range(2):
                    sp.wait_ge(y_out[u], 16 * (NG // 2))

            @block.tensor
            def _(pe):
                pe.wait_ge(ld, 48)

                def up(g, u, k, f):
                    m = g * FC + f
                    if f == 0:
                        pe.wait_ge(in_t[u], 16 * (k + 1))
                    if beyond(m, 1):
                        pe.wait_ge(hid_ready, m - 1)
                    pe.matmul(ps_h[f % 2][:, :], w1[:, P * f:P * f + P], xt[:, u, :],
                              start=True, stop=True).then_inc(h_ready, 1)

                def down(g, u, k, f):
                    m = g * FC + f
                    pe.wait_ge(hid_ready, m + 1)
                    if f == 0 and beyond(k, 0):
                        pe.wait_ge(y_ready, g - 1)
                    for t in range(GP):
                        mm = pe.matmul(ps_y[u][:, t, :], hid[:, f % 2, P * t:P * t + P], w2[:, f, :],
                                       start=(f == 0 and t == 0), stop=(f == FC - 1), skip_group_check=True)
                    mm.then_inc(used, 1)

                def step(g, u, k, first, last):
                    for f in range(FC):
                        if f < FC - 1:
                            up(g, u, k, f + 1)
                        elif not last:
                            up(g + 1, 1 - u, k if u == 0 else k + 1, 0)
                        down(g, u, k, f)
                up(0, 0, 0, 0)
                over_groups(pe, step)

            @block.scalar
            def _(act):
                act.wait_ge(ld, 48)

                def step(g, u, k, first, last):
                    for f in range(FC):
                        m = g * FC + f
                        act.wait_ge(h_ready, m + 1)
                        if beyond(m, 1):
                            act.wait_ge(used, m - 1)
                        act.activation(hid[:, f % 2, :], ps_h[f % 2][:, :], ACT.Gelu,
                                       bias=b1[:, f:f + 1]).then_inc(hid_ready, 1)
                over_groups(act, step)

            @block.vector
            def _(dve):
                def step(g, u, k, first, last):
                    dve.wait_ge(used, FC * (g + 1))
                    dve.wait_ge(xb_ready, g + 1)
                    if beyond(k, 0):
                        dve.wait_ge(y_out[u], 16 * k)
                    dve.tensor_tensor(y[:, u], ps_y[u][:, :, :], xb[:, u], ALU.add).then_inc(y_ready, 1)
                over_groups(dve, step)

            @block.gpsimd
            def _(pool):
                def step(g, u, k, first, last):
                    pool.wait_ge(in_x[u], 16 * (k + 1))
                    if beyond(k, 0):
                        pool.wait_ge(y_ready, g - 1)
                    pool.tensor_tensor(xb[:, u], xr[:, u], b2[:, None, :].broadcast_to([P, GP, D]),
                                       ALU.add).then_inc(xb_ready, 1)
                over_groups(pool, step)
        n.clear()


def moe_phase(nc, c, tag, xt_src, x_src, w1_dram, b1_dram, w2_dram, out_tok, out_tr):
    with ExitStack() as ctx:
        n = Names(nc, ctx, tag)
        w1 = n.sb("w1", [P, E, FF])
        w2 = n.sb("w2", [P, E * FC, D])
        b1 = n.sb("b1", [P, E * FC])
        xt = n.sb("xt", [P, 2, GT])
        xr = n.sb("xr", [P, 2, GP, D])
        hid = n.sb("hid", [P, 2, GT])
        y = n.sb("y", [P, 2, GP, D])
        xo = n.sb("xo", [P, 2, GT])
        ct = n.sb("ct", [E, 2, GT])
        order = n.sb("order", [P, GP, E])
        r = {m: n.sb("r_" + m, [P, GP, E]) for m in ("lg", "sh", "ex", "p", "eq", "key", "m1", "rest", "m2", "t1")}
        r["cw"] = n.sb("r_cw", [P, 2, GP, E])
        s = {m: n.sb("s_" + m, [P, GP]) for m in ("mx", "sum", "inv", "p1", "k1", "p2", "k2", "dp", "ed", "den",
                                                  "w1", "w2")}
        ordi = n.sb("ordi", [P, GP, E], mybir.dt.int32)
        ps_h = [n.ps(f"ps_h{i}", [P, GT]) for i in range(2)]
        ps_y = [n.ps(f"ps_y{i}", [P, GP, D]) for i in range(2)]
        ps_r = n.ps("ps_r", [P, GT])
        ps_c = n.ps("ps_c", [P, GT])
        ps_b = n.ps("ps_b", [P, GP, D])
        ps_x = n.ps("ps_x", [P, GT])
        ld, ord_ready = n.sem("weights_loaded"), n.sem("order_ready")
        in_t = [n.sem(f"in_t{i}") for i in range(2)]
        in_x = [n.sem(f"in_x{i}") for i in range(2)]
        tok_out = [n.sem(f"tok_out{i}") for i in range(2)]
        tr_out = [n.sem(f"tr_out{i}") for i in range(2)]
        lg_ready, sh_ready, ex_ready = n.sem("logits_ready"), n.sem("shifted_ready"), n.sem("exp_ready")
        dp_ready, ed_ready, cw_ready = n.sem("dp_ready"), n.sem("ed_ready"), n.sem("cw_ready")
        c_ready, ct_ready, b_ready = n.sem("c_ready"), n.sem("ct_ready"), n.sem("b_ready")
        h_ready, hid_ready, used = n.sem("h_ready"), n.sem("hid_ready"), n.sem("hid_used")
        acc_ready, y_ready, chain = n.sem("acc_ready"), n.sem("y_ready"), n.sem("chain")
        x_ready, xo_ready = n.sem("x_ready"), n.sem("xo_ready")
        ln = LayerNorm(n, "ln3", y, c.row["ln3_g"], c.row["ln3_b"], c)
        ln2 = LayerNorm(n, "l1ln", ln.out, c.row["l1_ln1_g"], c.row["l1_ln1_b"], c)
        x_v = x_src.rearrange("(g t p) d -> g p t d", t=GP, p=P)
        tok_v = out_tok.rearrange("(g t p) d -> g p t d", t=GP, p=P)
        M = E * FC
        CHAIN = 21

        with nc.Block() as block:
            @block.sync
            def _(sp):
                sp.dma_start(w1[:, :, :], w1_dram.rearrange("e p f -> p e f")).then_inc(ld, 16)
                sp.dma_start(w2[:, :, :], w2_dram.rearrange("e (c p) d -> p (e c) d", p=P)).then_inc(ld, 16)
                sp.dma_start(b1[:, :], b1_dram).then_inc(ld, 16)

                def load(g, u, k):
                    if beyond(k, 0):
                        sp.wait_ge(acc_ready, (E + 1) * (g - 1))
                        sp.wait_ge(lg_ready, g - 1)
                    sp.dma_start(xt[:, u, :], xt_src[:, bass.ts(g, GT)]).then_inc(in_t[u], 16)
                    sp.dma_start(xr[:, u], x_v[bass.ds(g, 1)].rearrange("o p t d -> p (o t) d")).then_inc(in_x[u], 16)

                def store(g, u, k):
                    sp.wait_ge(ln.out_ready, g + 1)
                    sp.dma_start(tok_v[bass.ds(g, 1)].rearrange("o p t d -> p (o t) d"), ln.out[:, u]).then_inc(
                        tok_out[u], 16)
                    sp.wait_ge(xo_ready, g + 1)
                    sp.dma_start(out_tr[:, bass.ts(g, GT)], xo[:, u, :]).then_inc(tr_out[u], 16)

                def step(g, u, k, first, last):
                    if not first:
                        if not last:
                            load(g + 1, 1 - u, k if u == 0 else k + 1)
                        store(g - 1, 1 - u, k)
                load(0, 0, 0)
                load(1, 1, 0)
                over_groups(sp, step)
                store(NG - 1, 1, NG // 2)
                for u in range(2):
                    sp.wait_ge(tok_out[u], 16 * (NG // 2))
                    sp.wait_ge(tr_out[u], 16 * (NG // 2))

            @block.tensor
            def _(pe):
                pe.wait_ge(ld, 48)

                def logits(g, u, k):
                    pe.wait_ge(in_t[u], 16 * (k + 1))
                    if beyond(g, 0):
                        pe.wait_ge(chain, CHAIN * (g - 1) + 1)
                    for t in range(GP):
                        mm = pe.matmul(ps_r[:, E * t:E * t + E], xt[:, u, P * t:P * t + P], c.rw[:, :],
                                       start=True, stop=True)
                    mm.then_inc(lg_ready, 1)

                def biases(g, u, k):
                    pe.wait_ge(cw_ready, g + 1)
                    if beyond(g, 0):
                        pe.wait_ge(ct_ready, g)
                    for t in range(GP):
                        tr = pe.transpose(ps_c[0:E, P * t:P * t + P], r["cw"][:, u, t, :], c.ident[:, :])
                    tr.then_inc(c_ready, 1)

                def biases_out(g, u, k):
                    pe.wait_ge(ct_ready, g + 1)
                    if beyond(g, 0):
                        pe.wait_ge(acc_ready, (E + 1) * (g - 1) + 1)
                    for t in range(GP):
                        mm = pe.matmul(ps_b[:, t, :], ct[:, u, P * t:P * t + P], c.eb2[:, :], start=True, stop=True)
                    mm.then_inc(b_ready, 1)

                def up(g, u, k, f):
                    m = g * M + f
                    if f == 0:
                        pe.wait_ge(in_t[u], 16 * (k + 1))
                    if beyond(m, 1):
                        pe.wait_ge(hid_ready, m - 1)
                    pe.matmul(ps_h[f % 2][:, :], w1[:, f // FC, P * (f % FC):P * (f % FC) + P], xt[:, u, :],
                              start=True, stop=True).then_inc(h_ready, 1)

                def down(g, u, k, f):
                    m = g * M + f
                    e = f // FC
                    pe.wait_ge(hid_ready, m + 1)
                    if f % FC == 0:
                        if e >= 2:
                            pe.wait_ge(acc_ready, (E + 1) * g + e)
                        elif beyond(g, 0):
                            pe.wait_ge(acc_ready, (E + 1) * (g - 1) + E + e)
                    for t in range(GP):
                        mm = pe.matmul(ps_y[e % 2][:, t, :], hid[:, f % 2, P * t:P * t + P], w2[:, f, :],
                                       start=(f % FC == 0 and t == 0), stop=(f % FC == FC - 1),
                                       skip_group_check=True)
                    mm.then_inc(used, 1)

                def turn_x(g, u):
                    pe.wait_ge(ln2.out_ready, g + 1)
                    if beyond(g, 0):
                        pe.wait_ge(xo_ready, g)
                    for t in range(GP):
                        tr = pe.transpose(ps_x[:, P * t:P * t + P], ln2.out[:, u, t, :], c.ident[:, :])
                    tr.then_inc(x_ready, 1)

                def step(g, u, k, first, last):
                    k1 = k if u == 0 else k + 1
                    for f in range(M):
                        if f < M - 1:
                            up(g, u, k, f + 1)
                        elif not last:
                            up(g + 1, 1 - u, k1, 0)
                        down(g, u, k, f)
                        if f == 2 and not last:
                            logits(g + 1, 1 - u, k1)
                        if f == 20 and not last:
                            biases(g + 1, 1 - u, k1)
                        if f == 23 and not last:
                            biases_out(g + 1, 1 - u, k1)
                        if f == 16 and not first:
                            turn_x(g - 1, 1 - u)
                logits(0, 0, 0)
                biases(0, 0, 0)
                biases_out(0, 0, 0)
                up(0, 0, 0, 0)
                over_groups(pe, step)
                turn_x(NG - 1, 1)

            @block.scalar
            def _(act):
                act.wait_ge(ld, 48)

                def routing_exp(g):
                    act.wait_ge(sh_ready, g + 1)
                    act.activation(r["ex"][:, :, :], r["sh"][:, :, :], ACT.Exp).then_inc(ex_ready, 1)
                    act.wait_ge(dp_ready, g + 1)
                    act.activation(s["ed"][:, :], s["dp"][:, :], ACT.Exp).then_inc(ed_ready, 1)

                def copy_c(g, u, k):
                    act.wait_ge(c_ready, g + 1)
                    if beyond(k, 0):
                        act.wait_ge(b_ready, g - 1)
                    act.activation(ct[:, u, :], ps_c[0:E, :], ACT.Copy).then_inc(ct_ready, 1)

                def copy_x(g, u, k):
                    act.wait_ge(x_ready, g + 1)
                    if beyond(k, 0):
                        act.wait_ge(tr_out[u], 16 * k)
                    act.activation(xo[:, u, :], ps_x[:, :], ACT.Copy).then_inc(xo_ready, 1)

                def step(g, u, k, first, last):
                    k1 = k if u == 0 else k + 1
                    for f in range(M):
                        m = g * M + f
                        act.wait_ge(h_ready, m + 1)
                        if beyond(m, 1):
                            act.wait_ge(used, m - 1)
                        act.activation(hid[:, f % 2, :], ps_h[f % 2][:, :], ACT.Gelu,
                                       bias=b1[:, f:f + 1]).then_inc(hid_ready, 1)
                        if f == 10 and not last:
                            routing_exp(g + 1)
                        if f == 22 and not last:
                            copy_c(g + 1, 1 - u, k1)
                        if f == 18 and not first:
                            copy_x(g - 1, 1 - u, k if u == 1 else k - 1)
                routing_exp(0)
                copy_c(0, 0, 0)
                over_groups(act, step)
                copy_x(NG - 1, 1, NG // 2 - 1)

            @block.vector
            def _(dve):
                dve.wait_ge(ord_ready, 1)
                dve.tensor_scalar(order[:, :, :], ordi[:, :, :], -1.0, float(E), ALU.mult,
                                  ALU.add).then_inc(ord_ready, 1)
                dve.wait_ge(ord_ready, 2)

                def wide(a):
                    return a[:, :, None].broadcast_to([P, GP, E])

                def route(g, u, k):
                    step_no = [0]

                    def linked(ins):
                        step_no[0] += 1
                        ins.then_inc(chain, 1)
                        dve.wait_ge(chain, CHAIN * g + step_no[0])

                    dve.wait_ge(lg_ready, g + 1)
                    linked(dve.tensor_tensor(r["lg"][:, :, :], ps_r[:, 0:GP * E].rearrange("p (t e) -> p t e", t=GP),
                                             c.rb[:, None, :].broadcast_to([P, GP, E]), ALU.add))
                    linked(dve.tensor_reduce(s["mx"][:, :], r["lg"][:, :, :], AX.X, ALU.max))
                    dve.tensor_tensor(r["sh"][:, :, :], r["lg"][:, :, :], wide(s["mx"]),
                                      ALU.subtract).then_inc(sh_ready, 1)
                    dve.wait_ge(ex_ready, g + 1)
                    linked(dve.tensor_reduce(s["sum"][:, :], r["ex"][:, :, :], AX.X, ALU.add))
                    linked(dve.reciprocal(s["inv"][:, :], s["sum"][:, :]))
                    linked(dve.tensor_tensor(r["p"][:, :, :], r["ex"][:, :, :], wide(s["inv"]), ALU.mult))
                    rest = r["p"]
                    for p_n, k_n, m_n in (("p1", "k1", "m1"), ("p2", "k2", "m2")):
                        linked(dve.tensor_reduce(s[p_n][:, :], rest[:, :, :], AX.X, ALU.max))
                        linked(dve.tensor_tensor(r["eq"][:, :, :], rest[:, :, :], wide(s[p_n]), ALU.is_equal))
                        linked(dve.tensor_tensor(r["key"][:, :, :], r["eq"][:, :, :], order[:, :, :], ALU.mult))
                        linked(dve.tensor_reduce(s[k_n][:, :], r["key"][:, :, :], AX.X, ALU.max))
                        linked(dve.tensor_tensor(r[m_n][:, :, :], r["key"][:, :, :], wide(s[k_n]), ALU.is_equal))
                        if m_n == "m1":
                            linked(dve.scalar_tensor_tensor(r["rest"][:, :, :], r["m1"][:, :, :], -4.0,
                                                            r["p"][:, :, :], ALU.mult, ALU.add))
                            rest = r["rest"]
                    dve.tensor_tensor(s["dp"][:, :], s["p2"][:, :], s["p1"][:, :], ALU.subtract).then_inc(dp_ready, 1)
                    dve.wait_ge(ed_ready, g + 1)
                    linked(dve.tensor_scalar(s["den"][:, :], s["ed"][:, :], 1.0, None, ALU.add))
                    linked(dve.reciprocal(s["w1"][:, :], s["den"][:, :]))
                    linked(dve.tensor_tensor(s["w2"][:, :], s["ed"][:, :], s["w1"][:, :], ALU.mult))
                    linked(dve.tensor_tensor(r["t1"][:, :, :], r["m1"][:, :, :], wide(s["w1"]), ALU.mult))
                    linked(dve.tensor_tensor(r["m2"][:, :, :], r["m2"][:, :, :], wide(s["w2"]), ALU.mult))
                    if beyond(k, 0):
                        dve.wait_ge(acc_ready, (E + 1) * (g - 1))
                        dve.wait_ge(c_ready, g - 1)
                    dve.tensor_tensor(r["cw"][:, u], r["t1"][:, :, :], r["m2"][:, :, :], ALU.add).then_inc(cw_ready, 1)
                    assert step_no[0] == CHAIN, step_no[0]

                def start_acc(g, u, k):
                    dve.wait_ge(b_ready, g + 1)
                    dve.wait_ge(in_x[u], 16 * (k + 1))
                    dve.tensor_tensor(y[:, u], ps_b[:, :, :], xr[:, u], ALU.add).then_inc(acc_ready, 1)

                def step(g, u, k, first, last):
                    kp = k if u == 1 else k - 1
                    start_acc(g, u, k)
                    for e in range(E):
                        dve.wait_ge(used, g * M + FC * (e + 1))
                        dve.wait_ge(acc_ready, (E + 1) * g + e + 1)
                        for t in range(GP):
                            ins = dve.scalar_tensor_tensor(y[:, u, t, :], ps_y[e % 2][:, t, :], r["cw"][:, u, t, e:e + 1],
                                                           y[:, u, t, :], ALU.mult, ALU.add)
                        ins.then_inc(acc_ready, 1)
                        if e == 0 and not first:
                            ln.dve_scale(dve, g - 1, 1 - u, kp, first)
                        if e == 1 and not last:
                            route(g + 1, 1 - u, k if u == 0 else k + 1)
                        if e == 2 and not first:
                            ln2.dve_statistics(dve, g - 1, 1 - u, kp, ln.out_ready, g)
                        if e == 3 and not first:
                            ln2.dve_scale(dve, g - 1, 1 - u, kp, first)
                    ln.dve_statistics(dve, g, u, k, acc_ready, (E + 1) * (g + 1))
                route(0, 0, 0)
                over_groups(dve, step)
                ln.dve_scale(dve, NG - 1, 1, NG // 2 - 1, False)
                ln2.dve_statistics(dve, NG - 1, 1, NG // 2 - 1, ln.out_ready, NG)
                ln2.dve_scale(dve, NG - 1, 1, NG // 2 - 1, False)

            @block.gpsimd
            def _(pool):
                for t in range(GP):
                    ins = pool.iota(ordi[:, t, :], [[1, E]], base=0, channel_multiplier=0)
                ins.then_inc(ord_ready, 1)

                def free(g, u, k):
                    if beyond(k, 0):
                        pool.wait_ge(tok_out[u], 16 * k)
                        pool.wait_ge(ln2.z_ready, g - 1)

                def free2(g, u, k):
                    if beyond(k, 0):
                        pool.wait_ge(x_ready, g - 1)

                def norms(g, u, k):
                    ln.pool_gain(pool, g, u, k, False, free)
                    ln2.pool_rstd(pool, g, u, k, False)
                    ln2.pool_gain(pool, g, u, k, False, free2)

                def step(g, u, k, first, last):
                    if not first:
                        norms(g - 1, 1 - u, k if u == 1 else k - 1)
                    ln.pool_rstd(pool, g, u, k, first)
                over_groups(pool, step)
                norms(NG - 1, 1, NG // 2 - 1)
        n.clear()


def build(nc, d, out):
    def scratch(name, shape):
        return nc.dram_tensor(name, shape, F32).ap()
    x1, x1t = scratch("x1", (T, D)), scratch("x1t", (D, T))
    x2, x2t = scratch("x2", (T, D)), scratch("x2t", (D, T))
    x3, q3t = scratch("x3", (T, D)), scratch("q3t", (D, T))
    x4, x4t = scratch("x4", (T, D)), scratch("x4t", (D, T))
    ctxnt = scratch("ctxnt", (D, T))

    with ExitStack() as ctx:
        n = Names(nc, ctx, "")
        c = Consts()
        load_constants(nc, n, c, d)
        attention_phase(nc, c, "sa_", "sa", d["xt"], d["xt"], d["x"], x1, x1t, True,
                        c.row["ln1_g"], c.row["ln1_b"], False)
        attention_phase(nc, c, "ca_", "ca", x1t, d["ctxt"], x1, x2, x2t, False,
                        c.row["ln2_g"], c.row["ln2_b"], False)
        norm_phase(nc, c, "cn_", d["ctx"], ctxnt, c.row["l1_ln1_g"], c.row["l1_ln1_b"])
        moe_phase(nc, c, "moe_", x2t, x2, d["e_w1"], d["e_b1"], d["e_w2"], x3, q3t)
        attention_phase(nc, c, "l1_", "l1", q3t, ctxnt, x3, x4, x4t, False,
                        c.row["l1_ln2_g"], c.row["l1_ln2_b"], True)
        mlp_phase(nc, c, "mlp_", x4t, x4, d["l1_w1"], d["l1_b1"], d["l1_w2"], c.row["l1_b2"], out)


class Consts:
    pass


_SHORT = {"x": "x", "ctx_1024": "ctx", "L0_xattn_router_w": "rw", "L0_xattn_router_b": "rb"}


def kernel(**inputs):
    import numpy as _np
    import concourse.bacc as _bacc
    from concourse import mybir as _mybir
    from concourse.bass_utils import run_bass_kernel_spmd as _run

    nc = _bacc.Bacc("TRN2", target_bir_lowering=False, num_devices=1)
    arrays, d = {}, {}
    laid = {}
    for name, a in inputs.items():
        a = _np.ascontiguousarray(a)
        if name in _SHORT:
            short = _SHORT[name]
        elif name.startswith("L0_xattn_"):
            short = name[len("L0_xattn_"):]
        else:
            short = "l1_" + name[len("L1_xattn_"):]
        if short in ("x", "ctx"):
            a = a.reshape(T, D)
            laid[short + "t"] = _np.ascontiguousarray(a.T)
        if short in ("e_b1", "l1_b1"):
            a = _np.ascontiguousarray(a.reshape(-1, P).T)
        laid[short] = a
    for short, a in laid.items():
        arrays["in_" + short] = a
        d[short] = nc.dram_tensor("in_" + short, a.shape, _mybir.dt.from_np(a.dtype), kind="ExternalInput").ap()
    out = nc.dram_tensor("out_0", (NBATCH, SEQ, D), _mybir.dt.float32, kind="ExternalOutput").ap()
    build(nc, d, out.rearrange("b s d -> (b s) d"))
    r = _run(nc, [arrays], core_ids=[0])
    return r.results[0]["out_0"]
```

```python
from contextlib import ExitStack

import concourse.bass as bass
from concourse import mybir

F32 = mybir.dt.float32
BF16 = mybir.dt.bfloat16
ALU = mybir.AluOpType
ACT = mybir.ActivationFunctionType
AX = mybir.AxisListType

P = 128
D = 128
NBATCH, SEQ = 128, 64
T = NBATCH * SEQ
H, HD = 16, 8
J = H // 2
GT = 512
GB = GT // SEQ
GP = GT // P
NG = T // GT
C = J // 2
E, FF = 8, 512
FC = FF // P
SCALE = float(HD) ** -0.5
EPS = 1e-5
I32, U32 = mybir.dt.int32, mybir.dt.uint32
TT = T // P
TU = 8
NT = -(-(2 * T // P + E - 1) // TU) * TU
HOT = 4
HB = 4
W1, B2 = 0, FF
B1, W2 = FF + D, FF + D + FC
W = W2 + FF
RT = 1024
RB = 4
MASKED = -1.0e30


def beyond(count, least):
    return not isinstance(count, int) or count > least


def before(count, end):
    return not isinstance(count, int) or count < end


class Names:

    def __init__(self, nc, ctx, prefix):
        self.nc, self.ctx, self.prefix = nc, ctx, prefix
        self.sems = []

    def sb(self, name, shape, dt=F32):
        return self.ctx.enter_context(self.nc.sbuf_tensor(self.prefix + name, shape, dt))

    def ps(self, name, shape, dt=F32):
        return self.ctx.enter_context(self.nc.psum_tensor(self.prefix + name, shape, dt))

    def sem(self, name):
        self.sems.append(self.ctx.enter_context(self.nc.semaphore(self.prefix + name)))
        return self.sems[-1]

    def clear(self):
        for s in self.sems:
            self.nc.gpsimd.sem_clear(s)
        self.nc.all_engine_barrier()


def over_groups(eng, step, peeled=1):
    for g in range(2 * peeled):
        step(g, g % 2, g // 2, g == 0, False)
    with eng.Fori(peeled, NG // 2 - 1) as k:
        for u in range(2):
            step(k * 2 + u, u, k, False, False)
    for u in range(2):
        step(NG - 2 + u, u, NG // 2 - 1, False, u == 1)


class LayerNorm:

    def __init__(self, n, name, y, gain, shift, consts):
        self.y, self.gain, self.shift, self.consts = y, gain, shift, consts
        self.tick = n.sb(name + "_tick", [1, 1])
        self.stats = n.sb(name + "_stats", [P, 2, GP, 6])
        self.mv = n.sb(name + "_mv", [P, 2, GP, 2])
        self.rstd = n.sb(name + "_rstd", [P, 2, GP])
        self.z = n.sb(name + "_z", [P, 2, GP, D])
        self.zg = n.sb(name + "_zg", [P, 2, GP, D])
        self.out = n.sb(name + "_out", [P, 2, GP, D])
        self.stats_ready = n.sem(name + "_stats_ready")
        self.mv_ready = n.sem(name + "_mv_ready")
        self.var_ready = n.sem(name + "_var_ready")
        self.rstd_ready = n.sem(name + "_rstd_ready")
        self.z_ready = n.sem(name + "_z_ready")
        self.zg_ready = n.sem(name + "_zg_ready")
        self.out_ready = n.sem(name + "_out_ready")

    def dve_statistics(self, dve, g, u, k, y_ready, count):
        dve.wait_ge(y_ready, count)
        for t in range(GP):
            ins = dve.bn_stats(self.stats[:, u, t, :], self.y[:, u, t, :])
        ins.then_inc(self.stats_ready, 1)

    def dve_moments(self, dve, g, u, k):
        dve.wait_ge(self.stats_ready, g + 1)
        if beyond(k, 0):
            dve.wait_ge(self.rstd_ready, g - 1)
        dve.memset(self.tick[:, :], 0.0)
        for t in range(GP):
            ins = dve.bn_aggr(self.mv[:, u, t, :], self.stats[:, u, t, :])
        ins.then_inc(self.mv_ready, 1)

    def pool_rstd(self, pool, g, u, k, first):
        pool.wait_ge(self.mv_ready, g + 1)
        if beyond(k, 0):
            pool.wait_ge(self.z_ready, g - 1)
        pool.tensor_tensor(self.rstd[:, u, :], self.mv[:, u, :, 1], self.consts.eps[:, 0:GP],
                           ALU.add).then_inc(self.var_ready, 1)
        pool.wait_ge(self.var_ready, g + 1)
        pool.tensor_tensor(self.rstd[:, u, :], self.rstd[:, u, :], self.consts.minus_half[:, 0:GP],
                           ALU.pow).then_inc(self.rstd_ready, 1)

    def dve_scale(self, dve, g, u, k, first):
        dve.wait_ge(self.rstd_ready, g + 1)
        dve.wait_ge(self.mv_ready, g + 1)
        if beyond(k, 0):
            dve.wait_ge(self.zg_ready, g - 1)
        for t in range(GP):
            ins = dve.tensor_scalar(self.z[:, u, t, :], self.y[:, u, t, :], self.mv[:, u, t, 0:1],
                                    self.rstd[:, u, t:t + 1], ALU.subtract, ALU.mult)
        ins.then_inc(self.z_ready, 1)

    def pool_gain(self, pool, g, u, k, first, free):
        gain = self.gain[:, None, :].broadcast_to([P, GP, D])
        shift = self.shift[:, None, :].broadcast_to([P, GP, D])
        pool.wait_ge(self.z_ready, g + 1)
        pool.tensor_tensor(self.zg[:, u], self.z[:, u], gain, ALU.mult).then_inc(self.zg_ready, 1)
        pool.wait_ge(self.zg_ready, g + 1)
        free(g, u, k)
        pool.tensor_tensor(self.out[:, u], self.zg[:, u], shift, ALU.add).then_inc(self.out_ready, 1)


def load_constants(nc, n, c, w):
    ld = n.sem("const_loaded")
    made = n.sem("const_made")
    dram = w
    c.ident = n.sb("ident", [P, P])
    c.minus_half = n.sb("minus_half", [P, 3 * GP])
    c.eps = n.sb("eps", [P, 3 * GP])
    c.side = n.sb("side", [P, 2])
    c.rowi = n.sb("rowi", [P, 1], I32)
    c.pari = n.sb("pari", [P, 1], I32)
    c.vx = n.sb("vx", [P, 2, GB, C, D])
    c.kx = n.sb("kx", [P, 2, J, GT])
    c.identb = n.sb("identb", [P, P], BF16)
    c.causal = n.sb("causal", [P, SEQ], BF16)
    c.mat, c.col, c.row = {}, {}, {}
    for name in ("sa_wq", "sa_wk", "sa_wv", "sa_wo", "ca_wq", "ca_wk", "ca_wv", "ca_wo", "l1_wq", "l1_wk",
                 "l1_wv", "l1_wo"):
        c.mat[name] = n.sb(name, [P, D])
    for name in ("sa_bq", "sa_bk", "sa_bv", "ca_bq", "ca_bk", "ca_bv", "l1_bq", "l1_bk", "l1_bv",
                 "l1_ln1_g", "l1_ln1_b"):
        c.col[name] = n.sb(name, [P, 1])
    for name in ("sa_bo", "ca_bo", "l1_bo", "ln1_g", "ln1_b", "ln2_g", "ln2_b", "ln3_g", "ln3_b",
                 "l1_ln2_g", "l1_ln2_b", "l1_b2"):
        c.row[name] = n.sb(name, [P, D])
    c.rw = n.sb("rw", [P, E])
    c.rb = n.sb("rb", [P, E])
    c.bqm = n.sb("bqm", [P, 3, 2])
    nloads = len(c.mat) + len(c.col) + len(c.row) + 2

    shifted = n.sem("shifted")
    with nc.psum_tensor("bias_gain", [P, 3], F32) as bg, nc.Block() as block:
        @block.sync
        def _(sp):
            for name, t in c.mat.items():
                sp.dma_start(t[:, :], dram[name]).then_inc(ld, 16)
            for name, t in c.col.items():
                sp.dma_start(t[:, :], dram[name].rearrange("(p o) -> p o", o=1)).then_inc(ld, 16)
            for name, t in c.row.items():
                sp.dma_start(t[:, :], dram[name].rearrange("(o d) -> o d", o=1).broadcast_to([P, D])).then_inc(ld, 16)
            sp.dma_start(c.rw[:, :], dram["rw"]).then_inc(ld, 16)
            sp.dma_start(c.rb[:, :], dram["rb"].rearrange("(o d) -> o d", o=1).broadcast_to([P, E])).then_inc(ld, 16)
            sp.wait_ge(ld, 16 * nloads)

        @block.tensor
        def _(pe):
            pe.wait_ge(ld, 16 * nloads)
            for i, name in enumerate(("q", "k", "v")):
                mm = pe.matmul(bg[:, i:i + 1], c.mat["l1_w" + name][:, :], c.col["l1_ln1_b"][:, 0:1],
                               start=True, stop=True)
            mm.then_inc(shifted, 1)

        @block.gpsimd
        def _(pool):
            pool.memset(c.minus_half[:, :], -0.5)
            pool.memset(c.eps[:, :], EPS)
            pool.memset(c.ident[:, :], 0.0).then_inc(made, 1)
            pool.memset(c.causal[:, :], 0.0).then_inc(made, 1)
            pool.iota(c.rowi[:, :], [[0, 1]], base=0, channel_multiplier=1).then_inc(made, 1)
            pool.wait_ge(made, 3)
            pool.affine_select(out=c.ident[:, :], in_=c.ident[:, :], compare_op=ALU.not_equal, fill=1.0, base=0,
                               pattern=[[-1, P]], channel_multiplier=1).then_inc(made, 1)
            for a in range(2):
                pool.wait_ge(made, 4 + a)
                pool.affine_select(out=c.causal[64 * a:64 * a + 64, :], in_=c.causal[64 * a:64 * a + 64, :],
                                   compare_op=ALU.is_ge, fill=MASKED, base=0, pattern=[[-1, SEQ]],
                                   channel_multiplier=1).then_inc(made, 1)

        @block.vector
        def _(dve):
            dve.memset(c.vx[:, :, :, :, :], 0.0)
            dve.memset(c.kx[:, :, :, :], 0.0)
            dve.wait_ge(made, 6)
            dve.tensor_copy(c.identb[:, :], c.ident[:, :])
            dve.tensor_scalar(c.pari[:, :], c.rowi[:, :], 3, 1, ALU.logical_shift_right,
                              ALU.bitwise_and).then_inc(made, 1)
            dve.wait_ge(made, 7)
            dve.tensor_copy(c.side[:, 1:2], c.pari[:, :]).then_inc(made, 1)
            dve.wait_ge(made, 8)
            dve.tensor_scalar(c.side[:, 0:1], c.side[:, 1:2], -1.0, 1.0, ALU.mult, ALU.add).then_inc(made, 1)
            dve.wait_ge(made, 9)
            dve.wait_ge(ld, 16 * nloads)
            dve.wait_ge(shifted, 1)
            for i, name in enumerate(("q", "k", "v")):
                bias = c.col["l1_b" + name]
                dve.tensor_tensor(bias[:, :], bias[:, :], bg[:, i:i + 1], ALU.add).then_inc(shifted, 1)
                dve.tensor_scalar(c.mat["l1_w" + name][:, :], c.mat["l1_w" + name][:, :],
                                  c.col["l1_ln1_g"][:, 0:1], None, ALU.mult)
            dve.wait_ge(shifted, 4)
            for i, name in enumerate(("sa_bq", "ca_bq", "l1_bq")):
                dve.tensor_scalar(c.bqm[:, i, :], c.side[:, :], c.col[name][:, 0:1], None, ALU.mult)


def attention_phase(nc, c, tag, layer, q_src, kv_src, x_src, out_tok, out_tr, causal, gain, shift, store_y):
    wq, wk, wv, wo = (c.mat[f"{layer}_w{m}"] for m in "qkvo")
    bk, bv = c.col[f"{layer}_bk"], c.col[f"{layer}_bv"]
    bo = c.row[f"{layer}_bo"]
    bqm = c.bqm[:, ("sa", "ca", "l1").index(layer), :]
    with ExitStack() as ctx:
        n = Names(nc, ctx, tag)
        qx = n.sb("qx", [P, 2, GT])
        kvx = n.sb("kvx", [P, 2, GB, 2, SEQ])
        xr = n.sb("xr", [P, 2, GP, D])
        xb = n.sb("xb", [P, 2, GP, D])
        kt = n.sb("kt", [P, 2, GT])
        qb = n.sb("qb", [P, 2, GB, 2, SEQ])
        mx = n.sb("mx", [P, 2, J])
        dd = n.sb("dd", [P, 2, J, SEQ])
        pr = n.sb("pr", [P, 2, J, SEQ])
        ph = n.sb("ph", [P, 2, J, SEQ // 2])
        pt = n.sb("pt", [P, 2, C, P])
        su = n.sb("su", [P, 2, 4, J])
        rc = n.sb("rc", [P, 2, 4, J])
        rcx = n.sb("rcx", [P, 2, 4, J, 2 * HD])
        rts = n.sb("rts", [P, 2, 4, 2, SEQ])
        on = n.sb("on", [P, 2, 4, 2, SEQ])
        ot = n.sb("ot", [P, 2, GT])
        y = n.sb("y", [P, 2, GP, D])
        xt = n.sb("xt", [P, 2, GT])
        bob = n.sb("bob", [P, D])
        bvb = n.sb("bvb", [P, P])
        ps_s = [n.ps(f"ps_s{i}", [P, J, SEQ]) for i in range(2)]
        ps_t = [n.ps(f"ps_t{i}", [P, C, P]) for i in range(2)]
        ps_o = [n.ps(f"ps_o{i}", [P, 4, 2, SEQ]) for i in range(2)]
        ps_g = [n.ps(f"ps_g{i}", [P, GT]) for i in range(2)]

        in_q = [n.sem(f"in_q{i}") for i in range(2)]
        in_kv = [n.sem(f"in_kv{i}") for i in range(2)]
        in_x = [n.sem(f"in_x{i}") for i in range(2)]
        kx_in = [n.sem(f"kx_in{i}") for i in range(2)]
        tok_out = [n.sem(f"tok_out{i}") for i in range(2)]
        tr_out = [n.sem(f"tr_out{i}") for i in range(2)]
        bvb_ready, bo_ready, bob_ready = n.sem("bvb_ready"), n.sem("bo_ready"), n.sem("bob_ready")
        k_ready, kt_ready = n.sem("k_ready"), n.sem("kt_ready")
        q_ready, qb_ready = n.sem("q_ready"), n.sem("qb_ready")
        v_ready, vx_ready = n.sem("v_ready"), n.sem("vx_ready")
        s_ready, mx_ready, d_ready = n.sem("s_ready"), n.sem("mx_ready"), n.sem("d_ready")
        p_ready, t_ready, pt_ready = n.sem("p_ready"), n.sem("t_ready"), n.sem("pt_ready")
        pv_ready, ph_ready, su_ready = n.sem("pv_ready"), n.sem("ph_ready"), n.sem("su_ready")
        rcx_ready = n.sem("rcx_ready")
        rc_ready, rt_ready, rts_ready = n.sem("rc_ready"), n.sem("rt_ready"), n.sem("rts_ready")
        on_ready, ot_ready, o_ready = n.sem("on_ready"), n.sem("ot_ready"), n.sem("o_ready")
        xb_ready, y_ready = n.sem("xb_ready"), n.sem("y_ready")
        x_ready, xt_ready = n.sem("x_ready"), n.sem("xt_ready")

        ln = LayerNorm(n, "ln", y, gain, shift, c)
        x_v = x_src.rearrange("(g t p) d -> g p t d", t=GP, p=P)
        tok_v = out_tok.rearrange("(g t p) d -> g p t d", t=GP, p=P)

        with nc.Block() as block:
            @block.sync
            def _(sp):
                def load(g, u, k):
                    if beyond(k, 0):
                        sp.wait_ge(v_ready, 2 * (g - 1))
                        sp.wait_ge(q_ready, g - 1)
                        sp.wait_ge(k_ready, g - 1)
                        sp.wait_ge(xb_ready, g - 1)
                    for e in range(2):
                        sp.dma_start(kvx[:, u, :, e, :], kv_src[:, bass.ts(g, GT)].rearrange(
                            "p (b q) -> p b q", b=GB)).then_inc(in_kv[u], 16)
                    sp.dma_start(qx[:, u, :], q_src[:, bass.ts(g, GT)]).then_inc(in_q[u], 16)
                    sp.dma_start(xr[:, u], x_v[bass.ds(g, 1)].rearrange("o p t d -> p (o t) d")).then_inc(in_x[u], 16)

                def spread(g, u, k):
                    if beyond(k, 0):
                        sp.wait_ge(s_ready, GB * (g - 1))
                    sp.wait_ge(kt_ready, g + 1)
                    for j in range(J):
                        sp.dma_start(c.kx[16 * j:16 * j + 16, u, j, :],
                                     kt[16 * j:16 * j + 16, u, :]).then_inc(kx_in[u], 16)

                def store(g, u, k):
                    if store_y:
                        sp.wait_ge(y_ready, g + 1)
                        src = y
                    else:
                        sp.wait_ge(ln.out_ready, g + 1)
                        src = ln.out
                    sp.dma_start(tok_v[bass.ds(g, 1)].rearrange("o p t d -> p (o t) d"), src[:, u]).then_inc(
                        tok_out[u], 16)
                    sp.wait_ge(xt_ready, g + 1)
                    sp.dma_start(out_tr[:, bass.ts(g, GT)], xt[:, u, :]).then_inc(tr_out[u], 16)

                load(0, 0, 0)
                load(1, 1, 0)
                spread(0, 0, 0)

                def step(g, u, k, first, last):
                    if before(k, NG // 2 - 1):
                        load(g + 2, u, k + 1)
                    if not last:
                        spread(g + 1, 1 - u, k if u == 0 else k + 1)
                    if not first:
                        store(g - 1, 1 - u, k)
                over_groups(sp, step)
                store(NG - 1, 1, NG // 2)
                for u in range(2):
                    sp.wait_ge(tok_out[u], 16 * (NG // 2))
                    sp.wait_ge(tr_out[u], 16 * (NG // 2))

            @block.tensor
            def _(pe):
                def scores(g, b, u, k):
                    nb = g * GB + b
                    if b == 0:
                        pe.wait_ge(kx_in[u], 16 * J * (k + 1))
                        pe.wait_ge(qb_ready, g + 1)
                    if beyond(nb, 1):
                        pe.wait_ge(d_ready, nb - 1)
                    mm = pe.matmul(ps_s[b % 2][:, :, :], qb[:, u, b, :, :], c.kx[:, u, :, 64 * b:64 * b + 64],
                                   start=True, stop=not causal)
                    if causal:
                        mm = pe.matmul(ps_s[b % 2][:, :, :], c.identb[:, :],
                                       c.causal[:, None, :].broadcast_to([P, J, SEQ]), start=False, stop=True)
                    mm.then_inc(s_ready, 1)

                def turn(g, b):
                    nb = g * GB + b
                    pe.wait_ge(p_ready, nb + 1)
                    if beyond(nb, 1):
                        pe.wait_ge(pt_ready, nb - 1)
                    for q in range(C):
                        tr = pe.transpose(ps_t[b % 2][:, q, :], pr[:, b % 2, 2 * q:2 * q + 2, :], c.ident[:, :])
                    tr.then_inc(t_ready, 1)

                def values(g, b, u):
                    nb = g * GB + b
                    quad = g * 2 + b // 4
                    pe.wait_ge(pt_ready, nb + 1)
                    if b == 0:
                        pe.wait_ge(vx_ready, 2 * g + 2)
                    if b % 4 == 0 and beyond(quad, 1):
                        pe.wait_ge(on_ready, quad - 1)
                    for q in range(C):
                        mm = pe.matmul(ps_o[b // 4][:, b % 4, :, :], c.vx[:, u, b, q, :], pt[:, b % 2, q, :],
                                       start=(q == 0), stop=(q == C - 1))
                    mm.then_inc(pv_ready, 1)

                def project_k(g, u, k, first):
                    pe.wait_ge(in_kv[u], 32 * (k + 1))
                    if not first:
                        pe.wait_ge(rts_ready, 2 * (g - 1) - 1)
                    pe.matmul(ps_g[0][:, :], wk[:, :], kvx[:, u, :, 0, :], start=True, stop=True).then_inc(k_ready, 1)

                def project_q(g, u, k, first):
                    pe.wait_ge(in_q[u], 16 * (k + 1))
                    pe.wait_ge(kt_ready, g + 1)
                    pe.matmul(ps_g[0][:, :], wq[:, :], qx[:, u, :], start=True, stop=True).then_inc(q_ready, 1)

                def project_v(g, u, half, bank):
                    for b in range(4):
                        mm = pe.matmul(ps_g[bank][:, D * b:D * b + D], kvx[:, u, 4 * half + b, :, :], wv[:, :],
                                       start=True, stop=True)
                    mm.then_inc(v_ready, 1)

                def reciprocals(quad, qu, bank):
                    pe.wait_ge(rcx_ready, quad + 1)
                    for b in range(4):
                        mm = pe.matmul(ps_g[bank][:, P * b:P * b + P],
                                       rcx[:, qu, b, :, :], c.ident[:, :],
                                       start=True, stop=True)
                    mm.then_inc(rt_ready, 1)

                def project_out(g, u):
                    pe.wait_ge(ot_ready, 2 * g + 2)
                    for t in range(GP):
                        mm = pe.matmul(ps_g[1][:, D * t:D * t + D], ot[:, u, P * t:P * t + P], wo[:, :],
                                       start=True, stop=True)
                    mm.then_inc(o_ready, 1)

                def turn_x(g, u):
                    pe.wait_ge(ln.out_ready, g + 1)
                    for t in range(GP):
                        tr = pe.transpose(ps_g[1][:, P * t:P * t + P], ln.out[:, u, t, :], c.ident[:, :])
                    tr.then_inc(x_ready, 1)

                pe.wait_ge(bvb_ready, 1)
                pe.matmul(ps_g[1][:, 0:D], bvb[:, :], wo[:, :], start=True, stop=True).then_inc(bo_ready, 1)
                project_k(0, 0, 0, True)
                project_q(0, 0, 0, True)
                pe.wait_ge(bob_ready, 1)
                project_v(0, 0, 0, 1)
                pe.wait_ge(qb_ready, 1)
                project_v(0, 0, 1, 0)
                scores(0, 0, 0, 0)

                def step(g, u, k, first, last):
                    k1 = k if u == 0 else k + 1
                    for b in range(GB):
                        if b < GB - 1:
                            scores(g, b + 1, u, k)
                        elif not last:
                            scores(g + 1, 0, 1 - u, k1)
                        if b > 0:
                            values(g, b - 1, u)
                        elif not first:
                            values(g - 1, GB - 1, 1 - u)
                        turn(g, b)
                        if b == 0 and not last:
                            if first:
                                pe.wait_ge(vx_ready, 2)
                            project_k(g + 1, 1 - u, k1, first)
                        if b == 1:
                            if not last:
                                project_q(g + 1, 1 - u, k1, first)
                            if not first:
                                if beyond(g, 1):
                                    pe.wait_ge(xt_ready, g - 1)
                                reciprocals(2 * g - 1, 1, 1)
                        if b == 2 and not last:
                            if first:
                                pe.wait_ge(vx_ready, 1)
                            else:
                                pe.wait_ge(rts_ready, 2 * g)
                            project_v(g + 1, 1 - u, 0, 1)
                        if b == 3 and not last:
                            pe.wait_ge(qb_ready, g + 2)
                            project_v(g + 1, 1 - u, 1, 0)
                        if b == 4 and not first:
                            if last:
                                pe.wait_ge(rts_ready, 2 * g)
                            else:
                                pe.wait_ge(vx_ready, 2 * g + 3)
                            project_out(g - 1, 1 - u)
                        if b == 5:
                            if last:
                                pe.wait_ge(rts_ready, 2 * g - 1)
                            else:
                                pe.wait_ge(vx_ready, 2 * g + 4)
                            reciprocals(2 * g, 0, 0)
                        if b == 7 and not first:
                            pe.wait_ge(y_ready, g)
                            turn_x(g - 1, 1 - u)
                over_groups(pe, step)
                values(NG - 1, GB - 1, 1)
                pe.wait_ge(xt_ready, NG - 1)
                reciprocals(2 * NG - 1, 1, 1)
                pe.wait_ge(rts_ready, 2 * NG)
                project_out(NG - 1, 1)
                pe.wait_ge(y_ready, NG)
                turn_x(NG - 1, 1)

            @block.scalar
            def _(act):
                def copy_q(g, u, k):
                    act.wait_ge(q_ready, g + 1)
                    if beyond(k, 0):
                        act.wait_ge(s_ready, GB * (g - 1))
                    for a in range(2):
                        ins = act.activation(qb[:, u, :, a, :], ps_g[0][:, :].rearrange("p (b q) -> p b q", b=GB),
                                             ACT.Identity, bias=bqm[:, a:a + 1], scale=c.side[:, a:a + 1])
                    ins.then_inc(qb_ready, 1)

                def copy_v(g, u, k, half, bank):
                    act.wait_ge(v_ready, 2 * g + half + 1)
                    if half == 0 and beyond(k, 0):
                        act.wait_ge(pv_ready, GB * (g - 1))
                    for r in range(2):
                        src = ps_g[bank][64 * r:64 * r + 64, :].rearrange(
                            "p (b c r m) -> p b c r m", b=4, c=C, r=2)[:, :, :, r, :]
                        dst = c.vx[64 * r:64 * r + 64, u, 4 * half:4 * half + 4, :, :].rearrange(
                            "p b c (e r m) -> p b (c e) r m", r=2, m=16)[:, :, 0:C * C:C + 1, r, :]
                        ins = act.activation(dst, src, ACT.Copy)
                    ins.then_inc(vx_ready, 1)

                def exponent(g, b):
                    nb = g * GB + b
                    act.wait_ge(d_ready, nb + 1)
                    if beyond(nb, 1):
                        act.wait_ge(t_ready, nb - 1)
                        act.wait_ge(ph_ready, nb - 1)
                    act.activation(pr[:, b % 2], dd[:, b % 2], ACT.Exp, scale=SCALE).then_inc(p_ready, 1)

                def copy_t(g, b):
                    nb = g * GB + b
                    act.wait_ge(t_ready, nb + 1)
                    if beyond(nb, 1):
                        act.wait_ge(pv_ready, nb - 1)
                    act.activation(pt[:, b % 2], ps_t[b % 2][:, :, :], ACT.Copy).then_inc(pt_ready, 1)

                def widen_r(quad, qu):
                    act.wait_ge(rc_ready, quad + 1)
                    if beyond(quad, 1):
                        act.wait_ge(rt_ready, quad - 1)
                    act.activation(rcx[:, qu], rc[:, qu, :, :, None].broadcast_to([P, 4, J, 2 * HD]),
                                   ACT.Copy).then_inc(rcx_ready, 1)

                def copy_r(quad, qu, bank):
                    act.wait_ge(rt_ready, quad + 1)
                    if beyond(quad, 1):
                        act.wait_ge(on_ready, quad - 1)
                    src = ps_g[bank][:, :].rearrange("p (b a q) -> p b a q", b=4, a=2)
                    for a in range(2):
                        ins = act.activation(rts[:, qu, :, a, :], src[:, :, a, :], ACT.Copy,
                                             scale=c.side[:, a:a + 1])
                    ins.then_inc(rts_ready, 1)

                def copy_x(g, u, k):
                    act.wait_ge(x_ready, g + 1)
                    if beyond(k, 0):
                        act.wait_ge(tr_out[u], 16 * k)
                    act.activation(xt[:, u, :], ps_g[1][:, :], ACT.Copy).then_inc(xt_ready, 1)

                copy_q(0, 0, 0)
                copy_v(0, 0, 0, 0, 1)
                copy_v(0, 0, 0, 1, 0)
                exponent(0, 0)

                def step(g, u, k, first, last):
                    k1 = k if u == 0 else k + 1
                    for b in range(GB):
                        copy_t(g, b)
                        if b < GB - 1:
                            exponent(g, b + 1)
                        elif not last:
                            exponent(g + 1, 0)
                        if b == 0 and not first:
                            widen_r(2 * g - 1, 1)
                        if b == 4:
                            widen_r(2 * g, 0)
                        if b == 1:
                            if not last:
                                copy_q(g + 1, 1 - u, k1)
                            if not first:
                                copy_r(2 * g - 1, 1, 1)
                        if b == 2 and not last:
                            copy_v(g + 1, 1 - u, k1, 0, 1)
                        if b == 3 and not last:
                            copy_v(g + 1, 1 - u, k1, 1, 0)
                        if b == 5:
                            copy_r(2 * g, 0, 0)
                        if b == 7 and not first:
                            copy_x(g - 1, 1 - u, k if u == 1 else k - 1)
                over_groups(act, step)
                widen_r(2 * NG - 1, 1)
                copy_r(2 * NG - 1, 1, 1)
                copy_x(NG - 1, 1, NG // 2 - 1)

            @block.vector
            def _(dve):
                def copy_k(g, u, k):
                    dve.wait_ge(k_ready, g + 1)
                    if beyond(k, 0):
                        dve.wait_ge(kx_in[u], 16 * J * k)
                    dve.tensor_scalar(kt[:, u, :], ps_g[0][:, :], bk[:, 0:1], None, ALU.add).then_inc(kt_ready, 1)

                def shift_scores(g, b):
                    nb = g * GB + b
                    dve.wait_ge(s_ready, nb + 1)
                    dve.tensor_reduce(mx[:, b % 2, :], ps_s[b % 2][:, :, :], AX.X, ALU.max).then_inc(mx_ready, 1)
                    dve.wait_ge(mx_ready, nb + 1)
                    if beyond(nb, 1):
                        dve.wait_ge(p_ready, nb - 1)
                    dve.tensor_tensor(dd[:, b % 2], ps_s[b % 2][:, :, :],
                                      mx[:, b % 2, :, None].broadcast_to([P, J, SEQ]),
                                      ALU.subtract).then_inc(d_ready, 1)

                def sum_up(g, b):
                    nb = g * GB + b
                    dve.wait_ge(ph_ready, nb + 1)
                    dve.tensor_reduce(su[:, b // 4, b % 4, :], ph[:, b % 2], AX.X, ALU.add).then_inc(su_ready, 1)

                def recip(quad, qu):
                    dve.wait_ge(su_ready, 4 * quad + 4)
                    if beyond(quad, 1):
                        dve.wait_ge(rcx_ready, quad - 1)
                    dve.reciprocal(rc[:, qu], su[:, qu]).then_inc(rc_ready, 1)

                def normalise(quad, qu):
                    dve.wait_ge(rts_ready, quad + 1)
                    dve.wait_ge(pv_ready, 4 * quad + 4)
                    if beyond(quad, 1):
                        dve.wait_ge(ot_ready, quad - 1)
                    dve.tensor_tensor(on[:, qu], ps_o[qu][:, :, :, :], rts[:, qu], ALU.mult).then_inc(on_ready, 1)

                def residual(g, u, k):
                    dve.wait_ge(o_ready, g + 1)
                    dve.wait_ge(xb_ready, g + 1)
                    if store_y and beyond(k, 0):
                        dve.wait_ge(tok_out[u], 16 * k)
                    dve.tensor_tensor(y[:, u], ps_g[1][:, :].rearrange("p (t d) -> p t d", t=GP), xb[:, u],
                                      ALU.add).then_inc(y_ready, 1)

                dve.tensor_copy(bvb[:, :], bv[:, 0:1].broadcast_to([P, P])).then_inc(bvb_ready, 1)
                dve.wait_ge(bo_ready, 1)
                dve.tensor_tensor(bob[:, :], ps_g[1][:, 0:D], bo[:, :], ALU.add).then_inc(bob_ready, 1)
                copy_k(0, 0, 0)
                shift_scores(0, 0)

                def step(g, u, k, first, last):
                    k1 = k if u == 0 else k + 1
                    kp = k if u == 1 else k - 1
                    for b in range(GB):
                        if b == 5 and not first:
                            ln.dve_moments(dve, g - 1, 1 - u, kp)
                        if b < GB - 1:
                            shift_scores(g, b + 1)
                        elif not last:
                            shift_scores(g + 1, 0)
                        sum_up(g, b)
                        if b == 0:
                            if not last:
                                copy_k(g + 1, 1 - u, k1)
                        if b == 2 and not first:
                            normalise(2 * g - 1, 1)
                        if b == 3:
                            recip(2 * g, 0)
                        if b == 4 and not first:
                            residual(g - 1, 1 - u, kp)
                            ln.dve_statistics(dve, g - 1, 1 - u, kp, y_ready, g)
                        if b == 5 and not first:
                            ln.dve_scale(dve, g - 1, 1 - u, kp, first)
                        if b == 6:
                            normalise(2 * g, 0)
                        if b == 7:
                            recip(2 * g + 1, 1)
                over_groups(dve, step)
                normalise(2 * NG - 1, 1)
                residual(NG - 1, 1, NG // 2 - 1)
                ln.dve_statistics(dve, NG - 1, 1, NG // 2 - 1, y_ready, NG)
                ln.dve_moments(dve, NG - 1, 1, NG // 2 - 1)
                ln.dve_scale(dve, NG - 1, 1, NG // 2 - 1, False)

            @block.gpsimd
            def _(pool):
                def halve(g, b):
                    nb = g * GB + b
                    pool.wait_ge(p_ready, nb + 1)
                    if beyond(nb, 1):
                        pool.wait_ge(su_ready, nb - 1)
                    pool.tensor_tensor(ph[:, b % 2], pr[:, b % 2, :, 0:SEQ // 2], pr[:, b % 2, :, SEQ // 2:SEQ],
                                       ALU.add).then_inc(ph_ready, 1)

                def add_bias(g, u, k):
                    pool.wait_ge(in_x[u], 16 * (k + 1))
                    if beyond(k, 0):
                        pool.wait_ge(y_ready, g - 1)
                    pool.tensor_tensor(xb[:, u], xr[:, u], bob[:, None, :].broadcast_to([P, GP, D]),
                                       ALU.add).then_inc(xb_ready, 1)

                def gather(quad, qu, g, u, k):
                    pool.wait_ge(on_ready, quad + 1)
                    if beyond(k, 0):
                        pool.wait_ge(o_ready, g - 1)
                    pool.tensor_tensor(ot[:, u, 256 * qu:256 * qu + 256].rearrange("p (b q) -> p b q", b=4),
                                       on[:, qu, :, 0, :], on[:, qu, :, 1, :], ALU.add).then_inc(ot_ready, 1)

                def out_free(g, u, k):
                    if beyond(k, 0):
                        pool.wait_ge(x_ready, g - 1)
                        if not store_y:
                            pool.wait_ge(tok_out[u], 16 * k)

                pool.wait_ge(bob_ready, 1)
                add_bias(0, 0, 0)

                def step(g, u, k, first, last):
                    k1 = k if u == 0 else k + 1
                    kp = k if u == 1 else k - 1
                    for b in range(GB):
                        if b == 5 and not first:
                            ln.pool_rstd(pool, g - 1, 1 - u, kp, first)
                        halve(g, b)
                        if b == 2 and not first:
                            gather(2 * g - 1, 1, g - 1, 1 - u, kp)
                        if b == 4 and not last:
                            add_bias(g + 1, 1 - u, k1)
                        if b == 6 and not first:
                            ln.pool_gain(pool, g - 1, 1 - u, kp, first, out_free)
                        if b == 7:
                            gather(2 * g, 0, g, u, k)
                over_groups(pool, step)
                gather(2 * NG - 1, 1, NG - 1, 1, NG // 2 - 1)
                ln.pool_rstd(pool, NG - 1, 1, NG // 2 - 1, False)
                ln.pool_gain(pool, NG - 1, 1, NG // 2 - 1, False, out_free)
        n.clear()


def route_phase(nc, c, r, tag, xt_src, experts):
    with ExitStack() as ctx:
        n = Names(nc, ctx, tag)
        rx = n.sb("rx", [P, RB, RT])
        ps_l = n.ps("ps_l", [P, TT, E])
        ps_rank = n.ps("ps_rank", [P, TT, E])
        ps_tot = n.ps("ps_tot", [P, TT, E])
        ps_tok = n.ps("ps_tok", [P, NT])
        w = {m: n.sb("w_" + m, [P, TT, E]) for m in ("lg", "sh", "ex", "p", "eq", "key", "m1", "rest", "m2", "both",
                                                     "slot")}
        v = {m: n.sb("v_" + m, [P, TT]) for m in ("mx", "sum", "inv", "p1", "k1", "p2", "k2", "dp", "ed", "den")}
        order = n.sb("order", [P, TT, E])
        tot = n.sb("tot", [P, E, TT])
        keep = n.sb("keep", [P, E, TT])
        above = n.sb("above", [P, E, TT])
        start = n.sb("start", [P, E, TT])
        ce = {m: n.sb("ce_" + m, [P, E]) for m in ("rows", "tiles", "end", "base", "one")}
        cei = n.sb("cei", [P, E], I32)
        sloti = n.sb("sloti", [P, 2, TT], I32)
        rowi = n.sb("rowi", [P, 2, 2, TT], I32)
        rowf = n.sb("rowf", [P, 2, 2, TT])
        slotf = n.sb("slotf", [P, 2, TT])
        tri = n.sb("tri", [P, P])
        ones = n.sb("ones", [P, P])
        numi = n.sb("numi", [P, NT], I32)
        num = n.sb("num", [P, NT])
        toki = n.sb("toki", [P, TT], I32)
        tok = n.sb("tok", [P, TT])
        after = n.sb("after", [1, NT, E])
        expf = n.sb("expf", [1, NT])
        tok2 = n.sb("tok2", [P, 2 * TT])
        row_hot = n.sb("row_hot", [P, HOT, P])
        tile_hot = n.sb("tile_hot", [P, HOT, NT])
        in_r = [n.sem(f"in_r{i}") for i in range(RB)]
        lg_ready, made, chain, work_ready = n.sem("lg_ready"), n.sem("made"), n.sem("chain"), n.sem("work_ready")
        exp_done, both_ready, rank_ready = n.sem("exp_done"), n.sem("both_ready"), n.sem("rank_ready")
        hot_ready, hot_used = n.sem("hot_ready"), n.sem("hot_used")
        with nc.Block() as block:
            @block.sync
            def _(sp):
                def load(g, u):
                    if beyond(g, RB - 1):
                        sp.wait_ge(lg_ready, g - RB + 1)
                    sp.dma_start(rx[:, u, :], xt_src[:, bass.ts(g, RT)]).then_inc(in_r[u], 16)
                for u in range(RB):
                    load(u, u)
                with sp.Fori(1, T // RT // RB) as k:
                    for u in range(RB):
                        load(k * RB + u, u)
                sp.dma_start(r.experts[:, :, W1:W1 + FF], experts[0].rearrange("e p f -> p e f")).then_inc(
                    r.loaded, 16)
                sp.dma_start(r.experts[:, :, B1:B1 + FC], experts[1].rearrange("p (e c) -> p e c", e=E)).then_inc(
                    r.loaded, 16)
                for e in range(E):
                    sp.dma_start(r.experts[:, e, W2:W2 + FF].rearrange("p (c d) -> p c d", c=FC),
                                 experts[2][e].rearrange("(c p) d -> p c d", p=P)).then_inc(r.loaded, 16)
                sp.dma_start(r.experts[:, :, B2:B2 + D], experts[3].rearrange("(o e) d -> o e d", o=1).broadcast_to(
                    [P, E, D])).then_inc(r.loaded, 16)

            @block.tensor
            def _(pe):
                def logits(g, u, k):
                    pe.wait_ge(in_r[u], 16 * (k + 1))
                    for t in range(RT // P):
                        mm = pe.matmul(ps_l[:, bass.ds(g * (RT // P) + t, 1), :], rx[:, u, P * t:P * t + P],
                                       c.rw[:, :], start=True, stop=True)
                    mm.then_inc(lg_ready, 1)
                for u in range(RB):
                    logits(u, u, 0)
                with pe.Fori(1, T // RT // RB) as k:
                    for u in range(RB):
                        logits(k * RB + u, u, k)

                pe.wait_ge(both_ready, 1)
                pe.matmul(ps_rank[:, :, :], tri[:, :], w["both"][:, :, :], start=True, stop=True)
                pe.matmul(ps_tot[:, :, :], ones[:, :], w["both"][:, :, :], start=True, stop=True).then_inc(rank_ready, 1)

                def hot(m, s, first, last):
                    pe.wait_ge(hot_ready, m + 1)
                    pe.matmul(ps_tok[:, :], row_hot[:, s, :], tile_hot[:, s, :], start=first,
                              stop=last).then_inc(hot_used, 1)
                for s in range(HOT):
                    hot(s, s, s == 0, False)
                with pe.Fori(1, 2 * TT // HOT - 1) as q:
                    for s in range(HOT):
                        hot(q * HOT + s, s, False, False)
                for s in range(HOT):
                    hot(2 * TT - HOT + s, s, False, s == HOT - 1)

            @block.scalar
            def _(act):
                act.wait_ge(work_ready, 1)
                act.activation(w["ex"][:, :, :], w["sh"][:, :, :], ACT.Exp).then_inc(exp_done, 1)
                act.wait_ge(work_ready, 2)
                act.activation(v["ed"][:, :], v["dp"][:, :], ACT.Exp).then_inc(exp_done, 1)

            @block.vector
            def _(dve):
                steps = [0]

                def linked(ins):
                    steps[0] += 1
                    ins.then_inc(chain, 1)
                    dve.wait_ge(chain, steps[0])

                def wide(a):
                    return a[:, :, None].broadcast_to([P, TT, E])

                dve.wait_ge(made, 5)
                dve.tensor_copy(tok[:, :], toki[:, :])
                linked(dve.tensor_copy(num[:, :], numi[:, :]))
                linked(dve.tensor_scalar(order[:, :, :], num[:, None, 0:E].broadcast_to([P, TT, E]), -1.0, float(E),
                                         ALU.mult, ALU.add))
                dve.wait_ge(lg_ready, T // RT)
                linked(dve.tensor_tensor(w["lg"][:, :, :], ps_l[:, :, :], c.rb[:, None, :].broadcast_to([P, TT, E]),
                                         ALU.add))
                linked(dve.tensor_reduce(v["mx"][:, :], w["lg"][:, :, :], AX.X, ALU.max))
                dve.tensor_tensor(w["sh"][:, :, :], w["lg"][:, :, :], wide(v["mx"]), ALU.subtract).then_inc(
                    work_ready, 1)
                dve.wait_ge(exp_done, 1)
                linked(dve.tensor_reduce(v["sum"][:, :], w["ex"][:, :, :], AX.X, ALU.add))
                linked(dve.reciprocal(v["inv"][:, :], v["sum"][:, :]))
                linked(dve.tensor_tensor(w["p"][:, :, :], w["ex"][:, :, :], wide(v["inv"]), ALU.mult))
                rest = w["p"]
                for p_n, k_n, m_n in (("p1", "k1", "m1"), ("p2", "k2", "m2")):
                    linked(dve.tensor_reduce(v[p_n][:, :], rest[:, :, :], AX.X, ALU.max))
                    linked(dve.tensor_tensor(w["eq"][:, :, :], rest[:, :, :], wide(v[p_n]), ALU.is_equal))
                    linked(dve.tensor_tensor(w["key"][:, :, :], w["eq"][:, :, :], order[:, :, :], ALU.mult))
                    linked(dve.tensor_reduce(v[k_n][:, :], w["key"][:, :, :], AX.X, ALU.max))
                    linked(dve.tensor_tensor(w[m_n][:, :, :], w["key"][:, :, :], wide(v[k_n]), ALU.is_equal))
                    if m_n == "m1":
                        linked(dve.scalar_tensor_tensor(w["rest"][:, :, :], w["m1"][:, :, :], -4.0,
                                                        w["p"][:, :, :], ALU.mult, ALU.add))
                        rest = w["rest"]
                dve.tensor_tensor(w["both"][:, :, :], w["m1"][:, :, :], w["m2"][:, :, :], ALU.add).then_inc(
                    both_ready, 1)
                dve.tensor_tensor(v["dp"][:, :], v["p2"][:, :], v["p1"][:, :], ALU.subtract).then_inc(work_ready, 1)
                dve.wait_ge(exp_done, 2)
                linked(dve.tensor_scalar(v["den"][:, :], v["ed"][:, :], 1.0, None, ALU.add))
                linked(dve.reciprocal(r.weight[:, 0, :], v["den"][:, :]))
                dve.tensor_tensor(r.weight[:, 1, :], v["ed"][:, :], r.weight[:, 0, :], ALU.mult)
                dve.wait_ge(rank_ready, 1)
                linked(dve.tensor_copy(tot[:, :, :], ps_tot[:, :, :].rearrange("p t e -> p e t")))
                linked(dve.tensor_tensor_scan(above[:, :, :].rearrange("p e t -> p (e t)"),
                                              keep[:, :, :].rearrange("p e t -> p (e t)"),
                                              tot[:, :, :].rearrange("p e t -> p (e t)"), 0.0, ALU.mult, ALU.add))
                linked(dve.tensor_scalar(ce["rows"][:, :], above[:, :, TT - 1], float(P - 1), None, ALU.add))
                linked(dve.tensor_copy(cei[:, :], ce["rows"][:, :]))
                linked(dve.tensor_scalar(cei[:, :], cei[:, :], 7, None, ALU.logical_shift_right))
                linked(dve.tensor_copy(ce["tiles"][:, :], cei[:, :]))
                linked(dve.tensor_tensor_scan(ce["end"][:, :], ce["one"][:, :], ce["tiles"][:, :], 0.0, ALU.mult,
                                              ALU.add))
                linked(dve.tensor_tensor(ce["base"][:, :], ce["end"][:, :], ce["tiles"][:, :], ALU.subtract))
                linked(dve.tensor_scalar(ce["base"][:, :], ce["base"][:, :], float(P), None, ALU.mult))
                linked(dve.tensor_tensor(start[:, :, :], above[:, :, :], tot[:, :, :], ALU.subtract))
                linked(dve.tensor_tensor(start[:, :, :], start[:, :, :],
                                         ce["base"][:, :, None].broadcast_to([P, E, TT]), ALU.add))
                linked(dve.tensor_tensor(w["slot"][:, :, :], ps_rank[:, :, :],
                                         start[:, :, :].rearrange("p e t -> p t e"), ALU.add))
                for choice, m_n in enumerate(("m1", "m2")):
                    linked(dve.tensor_tensor(w["eq"][:, :, :], w[m_n][:, :, :], w["slot"][:, :, :], ALU.mult))
                    linked(dve.tensor_reduce(slotf[:, choice, :], w["eq"][:, :, :], AX.X, ALU.add))
                linked(dve.tensor_copy(sloti[:, :, :], slotf[:, :, :]))
                dve.tensor_copy(r.slot[:, :, :], sloti[:, :, :])
                dve.tensor_scalar(rowi[:, 0], sloti[:, :, :], 7, None, ALU.logical_shift_right)
                linked(dve.tensor_scalar(rowi[:, 1], sloti[:, :, :], P - 1, None, ALU.bitwise_and))
                linked(dve.tensor_copy(rowf[:, :, :, :], rowi[:, :, :, :]))
                tile_of = rowf[:, 0].rearrange("p c t -> p (c t)")
                row_of = rowf[:, 1].rearrange("p c t -> p (c t)")

                linked(dve.tensor_tensor(after[:, :, :], num[0:1, :, None].broadcast_to([1, NT, E]),
                                         ce["end"][0:1, None, :].broadcast_to([1, NT, E]), ALU.is_ge))
                linked(dve.tensor_reduce(expf[:, :], after[:, :, :], AX.X, ALU.add))
                linked(dve.tensor_scalar(expf[:, :], expf[:, :], float(E - 1), None, ALU.min))
                dve.tensor_copy(r.expert[:, :], expf[:, :])

                def hot(m, s, early):
                    if not early:
                        dve.wait_ge(hot_used, m - HOT + 1)
                    dve.tensor_scalar(row_hot[:, s, :], num[:, 0:P], row_of[:, bass.ds(m, 1)], None, ALU.is_equal)
                    return dve.tensor_scalar(tile_hot[:, s, :], num[:, :], tile_of[:, bass.ds(m, 1)],
                                             tok2[:, bass.ds(m, 1)], ALU.is_equal, ALU.mult).then_inc(hot_ready, 1)
                linked(dve.tensor_copy(tok2[:, 0:TT], tok[:, :]))
                linked(dve.tensor_copy(tok2[:, TT:2 * TT], tok[:, :]))
                for s in range(HOT):
                    hot(s, s, True)
                with dve.Fori(1, 2 * TT // HOT) as q:
                    for s in range(HOT):
                        hot(q * HOT + s, s, False)
                dve.wait_ge(hot_used, 2 * TT)
                dve.tensor_copy(r.token[:, :], ps_tok[:, :])

            @block.gpsimd
            def _(pool):
                pool.iota(numi[:, :], [[1, NT]], base=0, channel_multiplier=0).then_inc(made, 1)
                pool.wait_ge(made, 1)
                pool.iota(toki[:, :], [[P, TT]], base=0, channel_multiplier=1).then_inc(made, 1)
                pool.memset(ones[:, :], 1.0)
                pool.memset(ce["one"][:, :], 1.0)
                pool.memset(tri[:, :], 1.0)
                pool.memset(keep[:, :, :], 1.0).then_inc(made, 1)
                pool.wait_ge(made, 3)
                pool.memset(keep[:, :, 0:1], 0.0).then_inc(made, 1)
                pool.wait_ge(made, 4)
                pool.affine_select(out=tri[:, :], in_=tri[:, :], compare_op=ALU.is_gt, fill=0.0, base=0,
                                   pattern=[[1, P]], channel_multiplier=-1).then_inc(made, 1)
        n.clear()


def mlp_phase(nc, c, tag, xt_src, x_src, w1_dram, b1_dram, w2_dram, b2, out_tok):
    with ExitStack() as ctx:
        n = Names(nc, ctx, tag)
        w1 = n.sb("w1", [P, FF])
        w2 = n.sb("w2", [P, FC, D])
        b1 = n.sb("b1", [P, FC])
        xt = n.sb("xt", [P, 2, GT])
        xr = n.sb("xr", [P, 2, GP, D])
        xb = n.sb("xb", [P, 2, GP, D])
        hid = n.sb("hid", [P, 2, GT])
        y = n.sb("y", [P, 2, GP, D])
        ps_h = [n.ps(f"ps_h{i}", [P, GT]) for i in range(2)]
        ps_y = [n.ps(f"ps_y{i}", [P, GP, D]) for i in range(2)]
        ld = n.sem("weights_loaded")
        in_t = [n.sem(f"in_t{i}") for i in range(2)]
        in_x = [n.sem(f"in_x{i}") for i in range(2)]
        y_out = [n.sem(f"y_out{i}") for i in range(2)]
        h_ready, hid_ready, o_ready = n.sem("h_ready"), n.sem("hid_ready"), n.sem("o_ready")
        used, xb_ready, y_ready = n.sem("hid_used"), n.sem("xb_ready"), n.sem("y_ready")
        x_v = x_src.rearrange("(g t p) d -> g p t d", t=GP, p=P)
        out_v = out_tok.rearrange("(g t p) d -> g p t d", t=GP, p=P)

        with nc.Block() as block:
            @block.sync
            def _(sp):
                sp.dma_start(w1[:, :], w1_dram).then_inc(ld, 16)
                sp.dma_start(w2[:, :, :], w2_dram.rearrange("(c p) d -> p c d", p=P)).then_inc(ld, 16)
                sp.dma_start(b1[:, :], b1_dram).then_inc(ld, 16)

                def load(g, u, k):
                    if beyond(k, 0):
                        sp.wait_ge(h_ready, FC * (g - 1))
                        sp.wait_ge(xb_ready, g - 1)
                    sp.dma_start(xt[:, u, :], xt_src[:, bass.ts(g, GT)]).then_inc(in_t[u], 16)
                    sp.dma_start(xr[:, u], x_v[bass.ds(g, 1)].rearrange("o p t d -> p (o t) d")).then_inc(in_x[u], 16)

                def step(g, u, k, first, last):
                    if not first and not last:
                        load(g + 1, 1 - u, k if u == 0 else k + 1)
                    sp.wait_ge(y_ready, g + 1)
                    sp.dma_start(out_v[bass.ds(g, 1)].rearrange("o p t d -> p (o t) d"), y[:, u]).then_inc(
                        y_out[u], 16)
                load(0, 0, 0)
                load(1, 1, 0)
                over_groups(sp, step)
                for u in range(2):
                    sp.wait_ge(y_out[u], 16 * (NG // 2))

            @block.tensor
            def _(pe):
                pe.wait_ge(ld, 48)

                def up(g, u, k, f):
                    m = g * FC + f
                    if f == 0:
                        pe.wait_ge(in_t[u], 16 * (k + 1))
                    if beyond(m, 1):
                        pe.wait_ge(hid_ready, m - 1)
                    pe.matmul(ps_h[f % 2][:, :], w1[:, P * f:P * f + P], xt[:, u, :],
                              start=True, stop=True).then_inc(h_ready, 1)

                def down(g, u, k, f):
                    m = g * FC + f
                    pe.wait_ge(hid_ready, m + 1)
                    if f == 0 and beyond(k, 0):
                        pe.wait_ge(y_ready, g - 1)
                    for t in range(GP):
                        mm = pe.matmul(ps_y[u][:, t, :], hid[:, f % 2, P * t:P * t + P], w2[:, f, :],
                                       start=(f == 0 and t == 0), stop=(f == FC - 1), skip_group_check=True)
                    mm.then_inc(used, 1)

                def step(g, u, k, first, last):
                    for f in range(FC):
                        if f < FC - 1:
                            up(g, u, k, f + 1)
                        elif not last:
                            up(g + 1, 1 - u, k if u == 0 else k + 1, 0)
                        down(g, u, k, f)
                up(0, 0, 0, 0)
                over_groups(pe, step)

            @block.scalar
            def _(act):
                act.wait_ge(ld, 48)

                def step(g, u, k, first, last):
                    for f in range(FC):
                        m = g * FC + f
                        act.wait_ge(h_ready, m + 1)
                        if beyond(m, 1):
                            act.wait_ge(used, m - 1)
                        act.activation(hid[:, f % 2, :], ps_h[f % 2][:, :], ACT.Gelu,
                                       bias=b1[:, f:f + 1]).then_inc(hid_ready, 1)
                over_groups(act, step)

            @block.vector
            def _(dve):
                def step(g, u, k, first, last):
                    dve.wait_ge(used, FC * (g + 1))
                    dve.wait_ge(xb_ready, g + 1)
                    if beyond(k, 0):
                        dve.wait_ge(y_out[u], 16 * k)
                    dve.tensor_tensor(y[:, u], ps_y[u][:, :, :], xb[:, u], ALU.add).then_inc(y_ready, 1)
                over_groups(dve, step)

            @block.gpsimd
            def _(pool):
                def step(g, u, k, first, last):
                    pool.wait_ge(in_x[u], 16 * (k + 1))
                    if beyond(k, 0):
                        pool.wait_ge(y_ready, g - 1)
                    pool.tensor_tensor(xb[:, u], xr[:, u], b2[:, None, :].broadcast_to([P, GP, D]),
                                       ALU.add).then_inc(xb_ready, 1)
                over_groups(pool, step)
        n.clear()


def over_tiles(eng, step):
    for s in range(TU):
        step(s, s, 0, True, False)
    with eng.Fori(1, NT // TU - 1) as q:
        for s in range(TU):
            step(q * TU + s, s, q, False, False)
    for s in range(TU):
        step(NT - TU + s, s, NT // TU - 1, False, True)


def expert_phase(nc, c, r, tag, x_src, out_rows):
    with ExitStack() as ctx:
        n = Names(nc, ctx, tag)
        ti = n.sb("ti", [P, TU], U32)
        tick = n.sb("tick", [1, 1])
        xg = n.sb("xg", [P, TU, D])
        xt = n.sb("xt", [P, HB, P])
        wt = n.sb("wt", [P, HB, W])
        hb = n.sb("hb", [P, 2, FC, P])
        hg = n.sb("hg", [P, 2, FC, P])
        y = n.sb("y", [P, TU, D])
        ps_x = [n.ps(f"ps_x{i}", [P, P]) for i in range(2)]
        ps_h = [n.ps(f"ps_h{i}", [P, FC, P]) for i in range(HB)]
        ps_y = [n.ps(f"ps_y{i}", [P, D]) for i in range(2)]
        xg_in = [n.sem(f"xg_in{i}") for i in range(TU)]
        y_out = [n.sem(f"y_out{i}") for i in range(TU)]
        copied, turned, xt_ready, wt_ready = n.sem("copied"), n.sem("turned"), n.sem("xt_ready"), n.sem("wt_ready")
        h_ready, hb_ready, hg_ready = n.sem("h_ready"), n.sem("hb_ready"), n.sem("hg_ready")
        down_ready, y_ready = n.sem("down_ready"), n.sem("y_ready")

        def inside(s, last, ahead):
            return not last or s + ahead < TU

        with nc.Block() as block:
            @block.sync
            def _(sp):
                def step(i, s, q, first, last):
                    sp.wait_ge(y_ready, i + 1)
                    sp.dma_start(out_rows[bass.ts(i, P), :], y[:, s, :]).then_inc(y_out[s], 16)
                over_tiles(sp, step)
                for s in range(TU):
                    sp.wait_ge(y_out[s], 16 * (NT // TU))

            @block.gpsimd
            def _(pool):
                def copy_number(i, s):
                    pool.tensor_copy(ti[:, s:s + 1], r.token[:, bass.ds(i, 1)]).then_inc(copied, 1)

                def step(i, s, q, first, last):
                    if not first or s == TU - 1:
                        pool.wait_ge(turned, i + 2 - TU)
                    pool.wait_ge(copied, i + 1)
                    pool.tensor_tensor(tick[:, :], c.eps[0:1, 0:1], c.eps[0:1, 0:1], ALU.add)
                    if inside(s, last, 1):
                        copy_number(i + 1, (s + 1) % TU)
                    pool.indirect_dma_start(
                        out=xg[:, s, :], out_offset=None, in_=x_src,
                        in_offset=bass.IndirectOffsetOnAxis(ap=ti[:, s:s + 1], axis=0)).then_inc(xg_in[s], 16)
                copy_number(0, 0)
                over_tiles(pool, step)

            @block.tensor
            def _(pe):
                def turn(i, s, q):
                    pe.wait_ge(xg_in[s], 16 * (q + 1))
                    if beyond(i, 1):
                        pe.wait_ge(xt_ready, i - 1)
                    pe.transpose(ps_x[s % 2][:, :], xg[:, s, :], c.ident[:, :]).then_inc(turned, 1)

                def up(i, s):
                    pe.wait_ge(xt_ready, i + 1)
                    pe.wait_ge(wt_ready, i + 1)
                    if beyond(i, HB - 1):
                        pe.wait_ge(hb_ready, i - HB + 1)
                    for f in range(FC):
                        mm = pe.matmul(ps_h[s % HB][:, f, :], wt[:, s % HB, W1 + P * f:W1 + P * f + P], xt[:, s % HB, :],
                                       start=True, stop=True)
                    mm.then_inc(h_ready, 1)

                def down(i, s):
                    pe.wait_ge(hg_ready, i + 1)
                    if beyond(i, 1):
                        pe.wait_ge(y_ready, i - 1)
                    for f in range(FC):
                        mm = pe.matmul(ps_y[s % 2][:, :], hg[:, s % 2, f, :], wt[:, s % HB, W2 + D * f:W2 + D * f + D],
                                       start=(f == 0), stop=(f == FC - 1))
                    mm.then_inc(down_ready, 1)

                def step(i, s, q, first, last):
                    if inside(s, last, 3):
                        turn(i + 3, (s + 3) % TU, q + (s + 3) // TU)
                    if inside(s, last, 2):
                        up(i + 2, (s + 2) % TU)
                    down(i, s)
                pe.wait_ge(r.loaded, 16 * (E + 3))
                for s in range(3):
                    turn(s, s, 0)
                for s in range(2):
                    up(s, s)
                over_tiles(pe, step)

            @block.scalar
            def _(act):
                def copy_x(i, s):
                    act.wait_ge(turned, i + 1)
                    if beyond(i, HB - 1):
                        act.wait_ge(h_ready, i - HB + 1)
                    act.activation(xt[:, s % HB, :], ps_x[s % 2][:, :], ACT.Copy).then_inc(xt_ready, 1)

                def step(i, s, q, first, last):
                    if inside(s, last, 3):
                        copy_x(i + 3, (s + 3) % TU)
                    act.wait_ge(hb_ready, i + 1)
                    if beyond(i, 1):
                        act.wait_ge(down_ready, i - 1)
                    act.activation(hg[:, s % 2], hb[:, s % 2], ACT.Gelu).then_inc(hg_ready, 1)
                for s in range(3):
                    copy_x(s, s)
                over_tiles(act, step)

            @block.vector
            def _(dve):
                def weights(i, s):
                    e = dve.value_load(r.expert[0:1, bass.ds(i, 1)], min_val=0, max_val=E - 1)
                    if beyond(i, HB - 1):
                        dve.wait_ge(y_ready, i - HB + 1)
                    dve.tensor_copy(wt[:, s % HB, None, :], r.experts[:, bass.ds(e, 1), :]).then_inc(wt_ready, 1)

                def bias_up(i, s):
                    dve.wait_ge(wt_ready, i + 1)
                    dve.wait_ge(h_ready, i + 1)
                    if beyond(i, 1):
                        dve.wait_ge(hg_ready, i - 1)
                    dve.tensor_tensor(hb[:, s % 2], ps_h[s % HB][:, :, :],
                                      wt[:, s % HB, B1:B1 + FC][:, :, None].broadcast_to([P, FC, P]), ALU.add).then_inc(hb_ready, 1)

                def bias_down(i, s, q):
                    dve.wait_ge(down_ready, i + 1)
                    if beyond(q, 0):
                        dve.wait_ge(y_out[s], 16 * q)
                    dve.tensor_tensor(y[:, s, :], ps_y[s % 2][:, :], wt[:, s % HB, B2:B2 + D],
                                      ALU.add).then_inc(y_ready, 1)

                def step(i, s, q, first, last):
                    if not first or s > 0:
                        bias_down(i - 1, (s - 1) % TU, q if s > 0 else q - 1)
                    if inside(s, last, 1):
                        bias_up(i + 1, (s + 1) % TU)
                    if inside(s, last, 3):
                        weights(i + 3, (s + 3) % TU)
                dve.wait_ge(r.loaded, 16 * (E + 3))
                for s in range(3):
                    weights(s, s)
                bias_up(0, 0)
                over_tiles(dve, step)
                bias_down(NT - 1, TU - 1, NT // TU - 1)
        n.clear()


def combine_phase(nc, c, r, tag, x_src, rows, ctx_src, x3_out, z4t_out, ct_out):
    with ExitStack() as ctx:
        n = Names(nc, ctx, tag)
        OWN, NEXT, CTX = range(3)
        xr = n.sb("xr", [P, 2, GP, D])
        cx = n.sb("cx", [P, 2, GP, D])
        sl = n.sb("sl", [P, 2, 2, GP], U32)
        wt = n.sb("wt", [P, 2, 2, GP])
        yg = n.sb("yg", [P, 2, 2, GP, D])
        y1 = n.sb("y1", [P, 2, GP, D])
        y = n.sb("y", [P, 2, GP, D])
        stats = n.sb("stats", [P, 2, 3, GP, 6])
        tick = n.sb("tick", [1, 1])
        tick_pool = n.sb("tick_pool", [1, 1])
        mv = n.sb("mv", [P, 2, 3 * GP, 2])
        std = n.sb("std", [P, 2, 3 * GP])
        guess = n.sb("guess", [P, 3 * GP])
        fac = n.sb("fac", [P, 3, 3 * GP])
        rstd = n.sb("rstd", [P, 2, 3 * GP])
        nb = n.sb("nb", [P, 2, 3 * GP])
        z3 = n.sb("z3", [P, 2, GP, D])
        zg3 = n.sb("zg3", [P, 2, GP, D])
        x3 = n.sb("x3", [P, 2, GP, D])
        z4 = n.sb("z4", [P, 2, GP, D])
        zc = n.sb("zc", [P, 2, GP, D])
        z4t = n.sb("z4t", [P, 2, GT])
        zct = n.sb("zct", [P, 2, GT])
        ps_4 = [n.ps(f"ps_4{i}", [P, GT]) for i in range(2)]
        ps_c = [n.ps(f"ps_c{i}", [P, GT]) for i in range(2)]
        in_x = [n.sem(f"in_x{i}") for i in range(2)]
        in_c = [n.sem(f"in_c{i}") for i in range(2)]
        yg_in = [n.sem(f"yg_in{i}") for i in range(2)]
        x3_stored = [n.sem(f"x3_stored{i}") for i in range(2)]
        z4_stored = [n.sem(f"z4_stored{i}") for i in range(2)]
        zc_stored = [n.sem(f"zc_stored{i}") for i in range(2)]
        copied, set_up = n.sem("copied"), n.sem("set_up")
        y1_ready, y_ready, stats_ready, mv_ready = n.sem("y1_ready"), n.sem("y_ready"), n.sem("stats_ready"), n.sem(
            "mv_ready")
        newton = n.sem("newton")
        std_ready, rstd_ready, nb_ready, ticked = n.sem("std_ready"), n.sem("rstd_ready"), n.sem("nb_ready"), n.sem(
            "ticked")
        z3_ready, zg3_ready, x3_ready = n.sem("z3_ready"), n.sem("zg3_ready"), n.sem("x3_ready")
        z4_ready, zc_ready = n.sem("z4_ready"), n.sem("zc_ready")
        t4_ready, tc_ready = n.sem("t4_ready"), n.sem("tc_ready")
        z4t_ready, zct_ready = n.sem("z4t_ready"), n.sem("zct_ready")

        def tokens(ap, g):
            return ap.rearrange("(g t p) d -> g p t d", t=GP, p=P)[bass.ds(g, 1)].rearrange("o p t d -> p (o t) d")

        def over_steps(eng, step):
            over_groups(eng, step, 2)
            step(NG, 0, NG // 2, False, True)
            step(NG + 1, 1, NG // 2, False, True)

        with nc.Block() as block:
            @block.sync
            def _(sp):
                def load_x(g, u, k):
                    if beyond(k, 0):
                        sp.wait_ge(y_ready, g - 1)
                    sp.dma_start(wt[:, u], r.weight[:, :, bass.ts(g, GP)]).then_inc(in_x[u], 16)
                    sp.dma_start(xr[:, u], tokens(x_src, g)).then_inc(in_x[u], 16)

                def load_c(g, u, k):
                    if beyond(k, 0):
                        sp.wait_ge(zc_ready, g - 1)
                    sp.dma_start(cx[:, u], tokens(ctx_src, g)).then_inc(in_c[u], 16)

                def step(g, u, k, first, last):
                    more = before(g, NG - 1) and not first
                    if more:
                        load_x(g + 1, 1 - u, k if u == 0 else k + 1)
                    if not first and before(g, NG + 1):
                        sp.wait_ge(x3_ready, g)
                        sp.dma_start(tokens(x3_out, g - 1), x3[:, 1 - u]).then_inc(x3_stored[1 - u], 16)
                    if more:
                        load_c(g + 1, 1 - u, k if u == 0 else k + 1)
                    if beyond(k, 0):
                        sp.wait_ge(z4t_ready, g - 1)
                        sp.dma_start(z4t_out[:, bass.ts(g - 2, GT)], z4t[:, u, :]).then_inc(z4_stored[u], 16)
                    if not first and before(g, NG + 1):
                        sp.wait_ge(zct_ready, g)
                        sp.dma_start(ct_out[:, bass.ts(g - 1, GT)], zct[:, 1 - u, :]).then_inc(zc_stored[1 - u], 16)
                for g in range(2):
                    load_x(g, g, 0)
                    load_c(g, g, 0)
                over_steps(sp, step)
                for u in range(2):
                    sp.wait_ge(x3_stored[u], 16 * (NG // 2))
                    sp.wait_ge(z4_stored[u], 16 * (NG // 2))
                    sp.wait_ge(zc_stored[u], 16 * (NG // 2))

            @block.gpsimd
            def _(pool):
                def copy_rows(g, u):
                    pool.tensor_copy(sl[:, u], r.slot[:, :, bass.ts(g, GP)]).then_inc(copied, 1)

                def fetch(g, u):
                    for choice in range(2):
                        for t in range(GP):
                            pool.indirect_dma_start(
                                out=yg[:, u, choice, t, :], out_offset=None, in_=rows,
                                in_offset=bass.IndirectOffsetOnAxis(ap=sl[:, u, choice, t:t + 1], axis=0)).then_inc(
                                    yg_in[u], 16)

                def tick():
                    pool.tensor_tensor(tick_pool[:, :], c.eps[0:1, 0:1], c.eps[0:1, 0:1], ALU.add).then_inc(ticked, 1)

                def step(g, u, k, first, last):
                    fetch(g + 1, 1 - u)
                    if before(g, NG - 2):
                        if not first:
                            pool.wait_ge(ticked, 2 * g)
                        pool.wait_ge(y_ready, g + 1)
                        tick()
                        copy_rows(g + 2, u)
                        pool.wait_ge(ticked, 2 * g + 1)
                        pool.wait_ge(copied, g + 3)
                        tick()
                copy_rows(0, 0)
                copy_rows(1, 1)
                pool.wait_ge(copied, 2)
                fetch(0, 0)
                for g in range(2):
                    step(g, g, 0, g == 0, False)
                with pool.Fori(1, NG // 2 - 1) as k:
                    for u in range(2):
                        step(k * 2 + u, u, k, False, False)
                step(NG - 2, 0, NG // 2 - 1, False, True)

            @block.tensor
            def _(pe):
                def step(g, u, k, first, last):
                    if beyond(k, 0):
                        pe.wait_ge(z4_ready, g - 1)
                        if beyond(k, 1):
                            pe.wait_ge(z4t_ready, g - 3)
                        for t in range(GP):
                            tr = pe.transpose(ps_4[u][:, P * t:P * t + P], z4[:, u, t, :], c.ident[:, :])
                        tr.then_inc(t4_ready, 1)
                    if not first and before(g, NG + 1):
                        pe.wait_ge(zc_ready, g)
                        if beyond(g, 2):
                            pe.wait_ge(zct_ready, g - 2)
                        for t in range(GP):
                            tr = pe.transpose(ps_c[1 - u][:, P * t:P * t + P], zc[:, 1 - u, t, :], c.ident[:, :])
                        tr.then_inc(tc_ready, 1)
                over_steps(pe, step)

            @block.scalar
            def _(act):
                def scale(out, src, u, which):
                    for t in range(GP):
                        ins = act.activation(out[:, t, :], src[:, t, :], ACT.Identity, bias=nb[:, u, GP * which + t:GP * which + t + 1],
                                             scale=rstd[:, u, GP * which + t:GP * which + t + 1])
                    return ins

                def step(g, u, k, first, last):
                    kp = k if u == 1 else k - 1
                    if not first:
                        act.wait_ge(nb_ready, g)
                    if not first and before(g, NG + 1):
                        if beyond(g, 2):
                            act.wait_ge(zg3_ready, g - 2)
                        scale(z3[:, 1 - u], y[:, 1 - u], 1 - u, OWN).then_inc(z3_ready, 1)
                    if beyond(k, 0):
                        if beyond(g, 3):
                            act.wait_ge(t4_ready, g - 3)
                        scale(z4[:, u], x3[:, u], 1 - u, NEXT).then_inc(z4_ready, 1)
                    if not first and before(g, NG + 1):
                        act.wait_ge(in_c[1 - u], 16 * (kp + 1))
                        if beyond(g, 2):
                            act.wait_ge(tc_ready, g - 2)
                        scale(zc[:, 1 - u], cx[:, 1 - u], 1 - u, CTX).then_inc(zc_ready, 1)
                    if beyond(k, 0):
                        act.wait_ge(t4_ready, g - 1)
                        if beyond(g, 3):
                            act.wait_ge(z4_stored[u], 16 * (k - 1))
                        act.activation(z4t[:, u, :], ps_4[u][:, :], ACT.Copy).then_inc(z4t_ready, 1)
                    if not first and before(g, NG + 1):
                        act.wait_ge(tc_ready, g)
                        if beyond(g, 2):
                            act.wait_ge(zc_stored[1 - u], 16 * kp)
                        act.activation(zct[:, 1 - u, :], ps_c[1 - u][:, :], ACT.Copy).then_inc(zct_ready, 1)
                    if before(g, NG + 1):
                        act.wait_ge(mv_ready, g + 1)
                        if beyond(k, 0):
                            act.wait_ge(rstd_ready, g - 1)
                        act.activation(std[:, u], mv[:, u, :, 1], ACT.Sqrt, bias=c.eps[:, 0:1]).then_inc(
                            std_ready, 1)
                over_steps(act, step)

            @block.vector
            def _(dve):
                def var_of(u):
                    return mv[:, u, :, 1]

                def gain_own(g, u):
                    dve.wait_ge(z3_ready, g + 1)
                    dve.tensor_tensor(zg3[:, u], z3[:, u], c.row["ln3_g"][:, None, :].broadcast_to([P, GP, D]),
                                      ALU.mult).then_inc(zg3_ready, 1)

                def shift_own(g, u, k):
                    dve.wait_ge(zg3_ready, g + 1)
                    if beyond(g, 1):
                        dve.wait_ge(x3_stored[u], 16 * k)
                        dve.wait_ge(z4_ready, g - 1)
                    dve.tensor_tensor(x3[:, u], zg3[:, u], c.row["ln3_b"][:, None, :].broadcast_to([P, GP, D]),
                                      ALU.add).then_inc(x3_ready, 1)

                def step(g, u, k, first, last):
                    kp = k if u == 1 else k - 1
                    add = before(g, NG)
                    if not first:
                        dve.wait_ge(std_ready, g)
                        if beyond(g, 2):
                            dve.wait_ge(zc_ready, g - 2)
                        dve.reciprocal(guess[:, :], std[:, 1 - u]).then_inc(newton, 1)
                    if add and before(g, NG + 1):
                        dve.wait_ge(yg_in[u], 16 * 2 * GP * (k + 1))
                        dve.wait_ge(in_x[u], 32 * (k + 1))
                    for t in range(GP):
                        if add:
                            ins = dve.scalar_tensor_tensor(y1[:, u, t, :], yg[:, u, 0, t, :], wt[:, u, 0, t:t + 1],
                                                           xr[:, u, t, :], ALU.mult, ALU.add)
                            if t == GP - 1:
                                ins.then_inc(y1_ready, 1)
                        if first:
                            continue
                        dve.wait_ge(newton, 4 * (g - 1) + t + 1)
                        if t == 0:
                            dve.scalar_tensor_tensor(fac[:, 0, :], var_of(1 - u), EPS, guess[:, :],
                                                     ALU.add, ALU.mult).then_inc(newton, 1)
                        elif t == 1:
                            dve.tensor_tensor(fac[:, 1, :], fac[:, 0, :], guess[:, :], ALU.mult).then_inc(newton, 1)
                        elif t == 2:
                            dve.tensor_scalar(fac[:, 2, :], fac[:, 1, :], -0.5, 1.5, ALU.mult, ALU.add).then_inc(
                                newton, 1)
                        else:
                            dve.tensor_tensor(rstd[:, 1 - u], guess[:, :], fac[:, 2, :], ALU.mult).then_inc(
                                rstd_ready, 1)
                    if not first:
                        dve.wait_ge(rstd_ready, g)
                        dve.scalar_tensor_tensor(nb[:, 1 - u], mv[:, 1 - u, :, 0], -1.0, rstd[:, 1 - u],
                                                 ALU.mult, ALU.mult).then_inc(nb_ready, 1)
                    if not before(g, NG + 1):
                        return
                    if add:
                        dve.wait_ge(in_c[u], 16 * (k + 1))
                        for t in range(GP):
                            dve.bn_stats(stats[:, u, CTX, t, :], cx[:, u, t, :])
                        dve.wait_ge(y1_ready, g + 1)
                        if beyond(g, 1):
                            dve.wait_ge(z3_ready, g - 1)
                        for t in range(GP):
                            ins = dve.scalar_tensor_tensor(y[:, u, t, :], yg[:, u, 1, t, :], wt[:, u, 1, t:t + 1],
                                                           y1[:, u, t, :], ALU.mult, ALU.add)
                        ins.then_inc(y_ready, 1)
                    if not first:
                        gain_own(g - 1, 1 - u)
                    if add:
                        dve.wait_ge(y_ready, g + 1)
                        for t in range(GP):
                            ins = dve.bn_stats(stats[:, u, OWN, t, :], y[:, u, t, :])
                    if not first:
                        shift_own(g - 1, 1 - u, kp)
                        dve.wait_ge(x3_ready, g)
                        for t in range(GP):
                            ins = dve.bn_stats(stats[:, u, NEXT, t, :], x3[:, 1 - u, t, :])
                    ins.then_inc(stats_ready, 1)
                    dve.wait_ge(stats_ready, g + 1)
                    dve.memset(tick[:, :], 0.0)
                    for which in range(3):
                        if (which == NEXT and first) or (which != NEXT and not add):
                            continue
                        for t in range(GP):
                            ins = dve.bn_aggr(mv[:, u, GP * which + t, :], stats[:, u, which, t, :])
                    ins.then_inc(mv_ready, 1)

                dve.memset(mv[:, 0, GP * NEXT:GP * NEXT + GP, :], 1.0).then_inc(set_up, 1)
                dve.wait_ge(set_up, 1)
                over_steps(dve, step)
        n.clear()


def build(nc, d, out):
    def scratch(name, shape):
        return nc.dram_tensor(name, shape, F32).ap()
    x1, x1t = scratch("x1", (T, D)), scratch("x1t", (D, T))
    x2, x2t = scratch("x2", (T, D)), scratch("x2t", (D, T))
    x3, z3t = scratch("x3", (T, D)), scratch("z3t", (D, T))
    x4, x4t = scratch("x4", (T, D)), scratch("x4t", (D, T))
    ctxzt = scratch("ctxzt", (D, T))
    rows = scratch("rows", (NT * P, D))

    with ExitStack() as ctx:
        n = Names(nc, ctx, "")
        c = Consts()
        load_constants(nc, n, c, d)
        r = Consts()
        r.weight = n.sb("weight", [P, 2, TT])
        r.slot = n.sb("slot", [P, 2, TT], U32)
        r.token = n.sb("token", [P, NT], U32)
        r.expert = n.sb("expert", [1, NT], I32)
        r.experts = n.sb("experts", [P, E, W])
        r.loaded = n.sem("experts_loaded")
        attention_phase(nc, c, "sa_", "sa", d["xt"], d["xt"], d["x"], x1, x1t, True,
                        c.row["ln1_g"], c.row["ln1_b"], False)
        attention_phase(nc, c, "ca_", "ca", x1t, d["ctxt"], x1, x2, x2t, False,
                        c.row["ln2_g"], c.row["ln2_b"], False)
        route_phase(nc, c, r, "rt_", x2t, (d["e_w1"], d["e_b1"], d["e_w2"], d["e_b2"]))
        expert_phase(nc, c, r, "ex_", x2, rows)
        combine_phase(nc, c, r, "cb_", x2, rows, d["ctx"], x3, z3t, ctxzt)
        attention_phase(nc, c, "l1_", "l1", z3t, ctxzt, x3, x4, x4t, False,
                        c.row["l1_ln2_g"], c.row["l1_ln2_b"], True)
        mlp_phase(nc, c, "mlp_", x4t, x4, d["l1_w1"], d["l1_b1"], d["l1_w2"], c.row["l1_b2"], out)


class Consts:
    pass


_SHORT = {"x": "x", "ctx_1024": "ctx", "L0_xattn_router_w": "rw", "L0_xattn_router_b": "rb"}


def kernel(**inputs):
    import numpy as _np
    import concourse.bacc as _bacc
    from concourse import mybir as _mybir
    from concourse.bass_utils import run_bass_kernel_spmd as _run

    nc = _bacc.Bacc("TRN2", target_bir_lowering=False, num_devices=1)
    arrays, d = {}, {}
    laid = {}
    for name, a in inputs.items():
        a = _np.ascontiguousarray(a)
        if name in _SHORT:
            short = _SHORT[name]
        elif name.startswith("L0_xattn_"):
            short = name[len("L0_xattn_"):]
        else:
            short = "l1_" + name[len("L1_xattn_"):]
        if short in ("x", "ctx"):
            a = a.reshape(T, D)
            laid[short + "t"] = _np.ascontiguousarray(a.T)
        if short in ("e_b1", "l1_b1"):
            a = _np.ascontiguousarray(a.reshape(-1, P).T)
        laid[short] = a
    for short, a in laid.items():
        arrays["in_" + short] = a
        d[short] = nc.dram_tensor("in_" + short, a.shape, _mybir.dt.from_np(a.dtype), kind="ExternalInput").ap()
    out = nc.dram_tensor("out_0", (NBATCH, SEQ, D), _mybir.dt.float32, kind="ExternalOutput").ap()
    build(nc, d, out.rearrange("b s d -> (b s) d"))
    r = _run(nc, [arrays], core_ids=[0])
    return r.results[0]["out_0"]
```
